# Optimizing a Trainium2 kernel written in Bass

```python
import numpy as np
import jax
import jax.numpy as jnp

def _softmax(x, axis=-1):
    return jax.nn.softmax(x, axis=axis)

def _gelu(x):
    return jax.nn.gelu(x, approximate=True)

def _silu(x):
    return jax.nn.silu(x)

def _sigmoid(x):
    return jax.nn.sigmoid(x)

def _layernorm(x, axis=-1, eps=1e-05):
    m = jnp.mean(x, axis=axis, keepdims=True)
    v = jnp.var(x, axis=axis, keepdims=True)
    return (x - m) / jnp.sqrt(v + eps)

def _scatter_add(tgt, idx, src, axis=0):
    return tgt.at[idx].add(src)

def _segment_sum(src, seg, n):
    return jax.ops.segment_sum(src, seg, n)
kernel_name = 'mk_xattn_ffn_d1_seqx_r4_064692'

def setup_inputs(seed: int=0):
    np.random.seed(seed)
    _w = jnp.asarray

    def _rec_inputs():
        import jax
        import jax.numpy as jnp
        _rk = jax.random.key(seed)
        x = -0.0003929 + 0.9999 * jax.random.normal(jax.random.fold_in(_rk, 1), (16, 256, 256), jnp.float32)
        _lenS = 256 - jax.random.randint(jax.random.fold_in(_rk, 7), (16,), 0, max(1, 256 // 4) + 1, jnp.int32)
        _lenS2 = 256 - jax.random.randint(jax.random.fold_in(_rk, 8), (16,), 0, max(1, 256 // 4) + 1, jnp.int32)
        _ctx_768P = jax.random.normal(jax.random.fold_in(_rk, 11), (16, 16, 192), jnp.float32)
        _ctx_768c = jax.random.dirichlet(jax.random.fold_in(_rk, 511), 0.3 * jnp.ones((16,), jnp.float32), (16, 256))
        _ctx_768t = jnp.einsum('bsk,bkd->bsd', _ctx_768c, _ctx_768P)
        _ctx_768t = _ctx_768t * jax.lax.rsqrt(jnp.mean(jnp.square(_ctx_768t)) + 1e-12) * 0.953939
        ctx_768 = 2.09791e-05 + 1.00001 * (_ctx_768t + 0.3 * jax.random.normal(jax.random.fold_in(_rk, 611), (16, 256, 192), jnp.float32))
        return (x, ctx_768)
    x, ctx_768 = _rec_inputs()

    def _L0_xattn_setup():
        import jax, jax.numpy as jnp
        import numpy as np
        EMBED_DIM = 256
        HIDDEN_DIM = 256
        NUM_HEADS = 16
        CONTEXT_DIM = 192
        HEAD_DIM = EMBED_DIM // NUM_HEADS
        SCALE = HEAD_DIM ** (-0.5)

        def _split_heads(x):
            b, n, _ = x.shape
            return x.reshape(b, n, NUM_HEADS, -1).transpose(0, 2, 1, 3)
        key = jax.random.key(seed)
        ks = jax.random.split(key, 7)
        B, N, M = (4, 1024, 256)
        tokens = jax.random.normal(ks[0], (B, N, HIDDEN_DIM), dtype=jnp.float32)
        context = jax.random.normal(ks[1], (B, M, CONTEXT_DIM), dtype=jnp.float32)
        Wq = jax.random.normal(ks[2], (HIDDEN_DIM, EMBED_DIM), dtype=jnp.float32) * HIDDEN_DIM ** (-0.5)
        Wk = jax.random.normal(ks[3], (CONTEXT_DIM, EMBED_DIM), dtype=jnp.float32) * CONTEXT_DIM ** (-0.5)
        Wv = jax.random.normal(ks[4], (CONTEXT_DIM, HIDDEN_DIM), dtype=jnp.float32) * CONTEXT_DIM ** (-0.5)
        Wo = jax.random.normal(ks[5], (HIDDEN_DIM, HIDDEN_DIM), dtype=jnp.float32) * HIDDEN_DIM ** (-0.5)
        bo = jax.random.normal(ks[6], (HIDDEN_DIM,), dtype=jnp.float32) * 0.01
        return {'tokens': tokens, 'context': context, 'Wq': Wq, 'Wk': Wk, 'Wv': Wv, 'Wo': Wo, 'bo': bo}
    _L0_xattn_all = _L0_xattn_setup()
    _L0_xattn_in = {k: v for k, v in _L0_xattn_all.items() if k in ('Wq', 'Wk', 'Wv', 'Wo', 'bo')}
    del _L0_xattn_all

    def _L0_ffn_setup():
        import jax, jax.numpy as jnp
        import numpy as np
        DIM = 256
        HIDDEN = 768
        SCALE = 1.0 / 127.0

        def _dequant(w_int, dtype):
            return w_int.astype(dtype) * jnp.asarray(SCALE, dtype)
        key = jax.random.key(seed)
        k_x, k_g, k_u, k_d = jax.random.split(key, 4)
        x = jax.random.normal(k_x, (4, 512, DIM), dtype=jnp.float32)
        w_gate = jax.random.randint(k_g, (HIDDEN, DIM), -127, 128, dtype=jnp.int32)
        w_up = jax.random.randint(k_u, (HIDDEN, DIM), -127, 128, dtype=jnp.int32)
        w_down = jax.random.randint(k_d, (DIM, HIDDEN), -127, 128, dtype=jnp.int32)
        return {'x': x, 'w_gate': w_gate, 'w_up': w_up, 'w_down': w_down}
    _L0_ffn_all = _L0_ffn_setup()
    _L0_ffn_in = {k: v for k, v in _L0_ffn_all.items() if k in ('w_gate', 'w_up', 'w_down')}
    del _L0_ffn_all
    return {'x': x, 'ctx_768': ctx_768, 'L0_xattn_Wq': _L0_xattn_in['Wq'], 'L0_xattn_Wk': _L0_xattn_in['Wk'], 'L0_xattn_Wv': _L0_xattn_in['Wv'], 'L0_xattn_Wo': _L0_xattn_in['Wo'], 'L0_xattn_bo': _L0_xattn_in['bo'], 'L0_ffn_w_gate': _L0_ffn_in['w_gate'], 'L0_ffn_w_up': _L0_ffn_in['w_up'], 'L0_ffn_w_down': _L0_ffn_in['w_down']}

def reference(x, ctx_768, L0_xattn_Wq, L0_xattn_Wk, L0_xattn_Wv, L0_xattn_Wo, L0_xattn_bo, L0_ffn_w_gate, L0_ffn_w_up, L0_ffn_w_down):
    import jax
    import jax.numpy as jnp

    def _L0_xattn_ref(tokens, context, Wq, Wk, Wv, Wo, bo):
        import jax, jax.numpy as jnp
        import numpy as np
        EMBED_DIM = 256
        HIDDEN_DIM = 256
        NUM_HEADS = 16
        CONTEXT_DIM = 192
        HEAD_DIM = EMBED_DIM // NUM_HEADS
        SCALE = HEAD_DIM ** (-0.5)

        def _split_heads(x):
            b, n, _ = x.shape
            return x.reshape(b, n, NUM_HEADS, -1).transpose(0, 2, 1, 3)
        Q = _split_heads(tokens @ Wq)
        K = _split_heads(context @ Wk)
        V = _split_heads(context @ Wv)
        scores = jnp.einsum('bhnd,bhmd->bhnm', Q, K) * SCALE
        attn = jax.nn.softmax(scores, axis=-1)
        out = jnp.einsum('bhnm,bhmd->bhnd', attn, V)
        b, h, n, d = out.shape
        out = out.transpose(0, 2, 1, 3).reshape(b, n, h * d)
        return out @ Wo + bo

    def _L0_ffn_ref(x, w_gate, w_up, w_down):
        import jax, jax.numpy as jnp
        import numpy as np
        DIM = 256
        HIDDEN = 768
        SCALE = 1.0 / 127.0

        def _dequant(w_int, dtype):
            return w_int.astype(dtype) * jnp.asarray(SCALE, dtype)
        wg = _dequant(w_gate, x.dtype)
        wu = _dequant(w_up, x.dtype)
        wd = _dequant(w_down, x.dtype)
        gate = jnp.einsum('bsd,hd->bsh', x, wg)
        up = jnp.einsum('bsd,hd->bsh', x, wu)
        h = jax.nn.silu(gate) * up
        return jnp.einsum('bsh,dh->bsd', h, wd)
    x = x + _L0_xattn_ref(_layernorm(x, axis=-1), ctx_768, L0_xattn_Wq, L0_xattn_Wk, L0_xattn_Wv, L0_xattn_Wo, L0_xattn_bo)
    x = x + _L0_ffn_ref(_layernorm(x, axis=-1), L0_ffn_w_gate, L0_ffn_w_up, L0_ffn_w_down)
    return x

_drawn_inputs = setup_inputs


def setup_inputs(seed=0):
    import zlib

    import numpy as np

    out = dict(_drawn_inputs(seed))
    spreads = {}
    factors = {'L0_xattn_bo': 4.235}
    for name, (base, spread) in spreads.items():
        noise = np.random.default_rng([zlib.crc32(name.encode()), seed]).standard_normal(out[name].shape)
        drawn = base * np.exp(spread * noise) if base else spread * noise
        out[name] = jnp.asarray(drawn.astype(out[name].dtype))
    for name, factor in factors.items():
        out[name] = (out[name] * factor).astype(out[name].dtype)
    return out
```

```python
import concourse.bass as bass
from concourse import mybir
from contextlib import ExitStack

F32 = mybir.dt.float32
F16 = mybir.dt.float16
I32 = mybir.dt.int32
ALU = mybir.AluOpType
ACT = mybir.ActivationFunctionType
AXX = mybir.AxisListType.X

B, N, D = 16, 256, 256
C = 192
H, HD = 16, 16
FF = 768
P = 128
PAIRS = H // 2
GROUPS = H // 4
U = 512
NU = B * N // U
UT = U // P
TILES = B * N // P
DK = D // P
FT = FF // P
EPS = 1e-5
WS = 16.0
SC = float(HD) ** -0.5
HS = 1.0 / 16.0
W_SCALE = 1.0 / 127.0
INT_EXACT = 2048.0
ROW_MAX = 63
RING = 4


def early(u):
    return isinstance(u, int) and u < 2


def block_program(nc, x, ctx_t, wq, wk, wv, wo, bo, wg, wu, wd, out):
    stack = ExitStack()
    with stack:
        def sb(name, shape, dt, where=stack):
            return where.enter_context(nc.sbuf_tensor(name, shape, dt))

        def sem(name, where=stack):
            return where.enter_context(nc.semaphore(name))

        x1 = sb("x1", [P, TILES, D], F32)
        ident = sb("ident", [P, P], F32)
        half = sb("half", [P, UT], F32)
        eps = sb("eps", [P, UT], F32)
        bo_bc = sb("bo_bc", [P, D], F32)
        wo_h = sb("wo_h", [P, DK, D], F16)
        wo_l = sb("wo_l", [P, DK, D], F16)
        q_dram = nc.dram_tensor("q_split", (B, 2, 2, P, N), F16, kind="Internal").ap()
        k_dram = nc.dram_tensor("k_split", (B, 2, 2, P, N), F16, kind="Internal").ap()

        shapes = ([P, DK, FF], [P, DK, FF], [P, FT, D])
        w32 = [sb(f"w32_{n}", shape, F32) for n, shape in enumerate(shapes)]
        w16 = [sb(f"w16_{n}", shape, F16) for n, shape in enumerate(shapes)]
        w_large = sb("w_large", [P, 1], I32)
        attn_scope = ExitStack()
        v_all = sb("v_all", [P, TILES, D], F32, attn_scope)
        q_stack = [sb(f"q_stack{i}", [P, PAIRS, N], F16, attn_scope) for i in range(RING)]
        k_stack = [sb(f"k_stack{i}", [P, PAIRS, N], F16, attn_scope) for i in range(RING)]
        v_pad = [sb(f"v_pad{i}", [P, 2, H, 32], F32, attn_scope) for i in range(RING)]

        project(nc, x, ctx_t, wq, wk, wv, wo, bo, x1, ident, half, eps, bo_bc, wo_h, wo_l, q_dram, k_dram,
                v_all, q_stack, k_stack, v_pad)
        attend(nc, x1, ident, bo_bc, wo_h, wo_l, q_dram, k_dram, v_all, q_stack, k_stack, v_pad,
               wg, wu, wd, w32, w16, w_large)
        attn_scope.close()
        feed(nc, out, x1, ident, half, eps, w32, w16, w_large)


def project(nc, x, ctx_t, wq, wk, wv, wo, bo, x1, ident, half, eps, bo_bc, wo_h, wo_l, q_dram, k_dram,
            v_all, q_stack, k_stack, v_pad):
    stack = ExitStack()
    with stack:
        def sb(name, shape, dt):
            return stack.enter_context(nc.sbuf_tensor(name, shape, dt))

        def sem(name):
            return stack.enter_context(nc.semaphore(name))

        w_raw = [sb(f"w_raw{i}", [P, DK, D], F32) for i in range(4)]
        wq_h, wq_l = sb("wq_h", [P, DK, D], F16), sb("wq_l", [P, DK, D], F16)
        wk_h, wk_l = sb("wk_h", [P, DK, D], F16), sb("wk_l", [P, DK, D], F16)
        wv_h, wv_l = sb("wv_h", [P, DK, D], F16), sb("wv_l", [P, DK, D], F16)
        ctx_raw = [sb(f"ctx_raw{i}", [P, DK, U], F32) for i in range(2)]
        ctx_h = [sb(f"ctx_h{i}", [P, DK, U], F16) for i in range(2)]
        ctx_l = [sb(f"ctx_l{i}", [P, DK, U], F16) for i in range(2)]
        stats = [sb(f"stats{i}", [P, UT, 6], F32) for i in range(2)]
        mean_var = [sb(f"mean_var{i}", [P, UT, 2], F32) for i in range(2)]
        rstd = [sb(f"rstd{i}", [P, UT], F32) for i in range(2)]
        var_eps = sb("var_eps", [P, UT], F32)
        xn = [sb(f"xn{i}", [P, UT, D], F32) for i in range(2)]
        xt_h = [sb(f"xt_h{i}", [P, DK, U], F16) for i in range(2)]
        xt_l = [sb(f"xt_l{i}", [P, DK, U], F16) for i in range(2)]
        q_h = [sb(f"q_h{i}", [P, 2, 2, N], F16) for i in range(2)]
        q_l = [sb(f"q_l{i}", [P, 2, 2, N], F16) for i in range(2)]
        k_h = [sb(f"k_h{i}", [P, 2, 2, N], F16) for i in range(2)]
        k_l = [sb(f"k_l{i}", [P, 2, 2, N], F16) for i in range(2)]

        ones = sb("ones", [2, N], F16)

        ps_x = stack.enter_context(nc.psum_tensor("ps_x", [P, DK, U], F32))
        ps_q = stack.enter_context(nc.psum_tensor("ps_q", [P, 2, U], F32))
        ps_k = stack.enter_context(nc.psum_tensor("ps_k", [P, 2, U], F32))
        ps_v = stack.enter_context(nc.psum_tensor("ps_v", [P, 2, U], F32))

        w_loaded, bo_loaded = sem("w_loaded"), sem("bo_loaded")
        x_loaded = [sem(f"x_loaded{i}") for i in range(2)]
        ctx_loaded = [sem(f"ctx_loaded{i}") for i in range(2)]
        q_stored = [sem(f"q_stored{i}") for i in range(2)]
        k_stored = [sem(f"k_stored{i}") for i in range(2)]
        consts_ready = sem("consts_ready")
        ident_zero = sem("ident_zero")
        w_hi, w_lo = sem("w_hi"), sem("w_lo")
        stats_done, mv_done, var_done, rstd_done, xn_done = (sem(n) for n in (
            "stats_done", "mv_done", "var_done", "rstd_done", "xn_done"))
        ctx_split = sem("ctx_split")
        ones_made, k_zeroed, ones_loaded = sem("ones_made"), sem("k_zeroed"), sem("ones_loaded")
        xt_ready, xt_hi, xt_lo = sem("xt_ready"), sem("xt_hi"), sem("xt_lo")
        q_ready, q_hi, q_lo = sem("q_ready"), sem("q_hi"), sem("q_lo")
        k_ready, k_hi, k_lo = sem("k_ready"), sem("k_hi"), sem("k_lo")
        v_ready, v_copied = sem("v_ready"), sem("v_copied")

        def walk(eng, step):
            for u in range(2):
                step(u, u, 0, lambda d: u + d >= 0)
            with eng.Fori(1, NU // 2 - 1) as j:
                for s in range(2):
                    step(2 * j + s, s, j, lambda d: True)
            for u in range(NU - 2, NU):
                step(u, u % 2, u // 2, lambda d: u + d < NU)

        block = stack.enter_context(nc.Block())

        @block.sync
        def _(sp):
            def load_unit(u, s):
                sp.dma_start(x1[:, bass.ds(UT * u, UT), :],
                             x[bass.ds(U * u, U), :].rearrange("(t p) d -> p t d", p=P)).then_inc(x_loaded[s], 16)

            def load_ctx(u, s):
                src = ctx_t[bass.ds(2 * u, 2), :, :].rearrange("b c t -> c b t")
                sp.dma_start(ctx_raw[s][:, 0, :].rearrange("c (b t) -> c b t", b=2),
                             src[0:P]).then_inc(ctx_loaded[s], 16)
                sp.dma_start(ctx_raw[s][0:C - P, 1, :].rearrange("c (b t) -> c b t", b=2),
                             src[P:C]).then_inc(ctx_loaded[s], 16)

            def store_unit(u, s):
                sp.wait_ge(k_hi, u + 1)
                sp.dma_start(k_dram[bass.ds(2 * u, 2), :, 0].rearrange("b e p t -> p (b e) t"),
                             k_h[s][:].rearrange("p b e t -> p (b e) t")).then_inc(k_stored[s], 16)
                sp.wait_ge(k_lo, 2 * u + 2)
                sp.dma_start(k_dram[bass.ds(2 * u, 2), :, 1].rearrange("b e p t -> p (b e) t"),
                             k_l[s][:].rearrange("p b e t -> p (b e) t")).then_inc(k_stored[s], 16)
                sp.wait_ge(q_hi, u + 1)
                sp.dma_start(q_dram[bass.ds(2 * u, 2), :, 0].rearrange("b e p t -> p (b e) t"),
                             q_h[s][:].rearrange("p b e t -> p (b e) t")).then_inc(q_stored[s], 16)
                sp.wait_ge(q_lo, 2 * u + 2)
                sp.dma_start(q_dram[bass.ds(2 * u, 2), :, 1].rearrange("b e p t -> p (b e) t"),
                             q_l[s][:].rearrange("p b e t -> p (b e) t")).then_inc(q_stored[s], 16)

            load_unit(0, 0)
            load_ctx(0, 0)
            for raw, src in ((w_raw[2], wk), (w_raw[3], wv)):
                sp.dma_start(raw[:, 0, :], src[0:P, :]).then_inc(w_loaded, 16)
                sp.dma_start(raw[0:C - P, 1, :], src[P:C, :]).then_inc(w_loaded, 16)
            sp.dma_start(w_raw[0][:], wq.rearrange("(k p) n -> p k n", p=P)).then_inc(w_loaded, 16)
            load_unit(1, 1)
            load_ctx(1, 1)
            sp.dma_start(w_raw[1][:], wo.rearrange("(k p) n -> p k n", p=P)).then_inc(w_loaded, 16)
            sp.dma_start(bo_bc[:], bo.partition_broadcast(P)).then_inc(bo_loaded, 16)
            sp.wait_ge(ones_made, 1)
            for r in range(RING):
                sp.wait_ge(k_zeroed, r + 1)
                sp.dma_start(k_stack[r][ROW_MAX:ROW_MAX + 65:64],
                             ones[:].unsqueeze(1).to_broadcast([2, PAIRS, N])).then_inc(ones_loaded, 16)
            def step(u, s, turn, has):
                if has(2):
                    sp.wait_ge(x_loaded[s], 16 * turn + 16)
                    load_unit(u + 2, s)
                    sp.wait_ge(ctx_split, 4 * u + 4)
                    load_ctx(u + 2, s)
                store_unit(u, s)

            walk(sp, step)
            sp.wait_ge(bo_loaded, 16)
            sp.wait_ge(ones_loaded, 16 * RING)
            for s in range(2):
                sp.wait_ge(q_stored[s], 32 * NU // 2)
                sp.wait_ge(k_stored[s], 32 * NU // 2)

        @block.gpsimd
        def _(pool):
            nc.gpsimd.memset(ident[:], 0.0).then_inc(ident_zero, 1)
            pool.wait_ge(ident_zero, 1)
            nc.gpsimd.affine_select(out=ident[:], in_=ident[:], compare_op=ALU.not_equal, fill=1.0, base=0,
                                    pattern=[[-1, P]], channel_multiplier=1).then_inc(consts_ready, 1)
            nc.gpsimd.memset(half[:], -0.5).then_inc(consts_ready, 1)
            nc.gpsimd.memset(eps[:], EPS).then_inc(consts_ready, 1)
            pool.wait_ge(consts_ready, 3)

            for r in range(RING):
                nc.gpsimd.memset(v_pad[r][:, :, :, HD:HD + 1], 1.0)
                nc.gpsimd.memset(v_pad[r][:, :, :, HD + 1:32], 0.0)

            def rstd_unit(u, s):
                pool.wait_ge(mv_done, u + 1)
                if not (isinstance(u, int) and u == 0):
                    pool.wait_ge(rstd_done, u)
                nc.gpsimd.tensor_tensor(var_eps[:], mean_var[s][:, :, 1], eps[:], ALU.add).then_inc(var_done, 1)
                pool.wait_ge(var_done, u + 1)
                nc.gpsimd.tensor_tensor(rstd[s][:], var_eps[:], half[:], ALU.pow).then_inc(rstd_done, 1)

            def split_ctx(u, s):
                for k, rows in ((0, P), (1, C - P)):
                    nc.gpsimd.tensor_copy(ctx_h[s][0:rows, k, :], ctx_raw[s][0:rows, k, :]).then_inc(ctx_split, 1)
                    pool.wait_ge(ctx_split, 4 * u + 2 * k + 1)
                    nc.gpsimd.tensor_tensor(ctx_l[s][0:rows, k, :], ctx_raw[s][0:rows, k, :],
                                            ctx_h[s][0:rows, k, :], ALU.subtract).then_inc(ctx_split, 1)

            pool.wait_ge(ctx_loaded[0], 32)
            split_ctx(0, 0)
            rstd_unit(0, 0)
            rstd_unit(1, 1)
            pool.wait_ge(ctx_loaded[1], 32)
            split_ctx(1, 1)
            for r in range(RING):
                nc.gpsimd.memset(q_stack[r][:].rearrange("p a t -> p (a t)").bitcast(I32), 0)

            def step(u, s, turn, has):
                if has(2):
                    pool.wait_ge(ctx_loaded[s], 32 * turn + 64)
                    pool.wait_ge(v_ready, u + 1)
                    rstd_unit(u + 2, s)
                    split_ctx(u + 2, s)

            walk(pool, step)

        @block.vector
        def _(dve):
            def stats_unit(u, s, turn):
                dve.wait_ge(x_loaded[s], 16 * (turn + 1))
                if not early(u):
                    dve.wait_ge(mv_done, u - 1)
                    dve.wait_ge(xn_done, u - 1)
                    dve.wait_ge(rstd_done, u - 1)
                for t in range(UT):
                    last = nc.vector.bn_stats(stats[s][:, t, :], x1[:, bass.ds(UT * u + t, 1), :].rearrange("p a d -> p (a d)"))
                last.then_inc(stats_done, 1)

            def aggregate_unit(u, s):
                for t in range(UT):
                    last = nc.vector.bn_aggr(mean_var[s][:, t, :], stats[s][:, t, :])
                last.then_inc(mv_done, 1)

            def normalise_unit(u, s):
                dve.wait_ge(rstd_done, u + 1)
                if not early(u):
                    dve.wait_ge(xt_ready, u - 1)
                for t in range(UT):
                    last = nc.vector.tensor_scalar(xn[s][:, t, :], x1[:, bass.ds(UT * u + t, 1), :].rearrange("p a d -> p (a d)"),
                                                   mean_var[s][:, t, 0:1], rstd[s][:, t:t + 1],
                                                   ALU.subtract, ALU.mult)
                last.then_inc(xn_done, 1)

            def low(dst, ps, hi, scale, done):
                nc.vector.scalar_tensor_tensor(out=dst, in0=ps, scalar=scale, in1=hi,
                                               op0=ALU.mult, op1=ALU.subtract).then_inc(done, 1)

            def xt_low(u, s):
                dve.wait_ge(xt_hi, u + 1)
                low(xt_l[s][:], ps_x[:], xt_h[s][:], 1.0, xt_lo)

            def k_low(u, s, turn):
                dve.wait_ge(k_hi, u + 1)
                if not early(u):
                    dve.wait_ge(k_stored[s], 32 * turn)
                for e in range(2):
                    low(k_l[s][:, :, e], ps_k[:, e].rearrange("p (b t) -> p b t", b=2), k_h[s][:, :, e], 1.0 / WS, k_lo)

            def q_low(u, s, turn):
                dve.wait_ge(q_hi, u + 1)
                if not early(u):
                    dve.wait_ge(q_stored[s], 32 * turn)
                for e in range(2):
                    low(q_l[s][:, :, e], ps_q[:, e].rearrange("p (b t) -> p b t", b=2), q_h[s][:, :, e], SC / WS, q_lo)

            nc.vector.memset(ones[:], 1.0).then_inc(ones_made, 1)
            for r in range(RING):
                nc.vector.memset(k_stack[r][:].rearrange("p a t -> p (a t)").bitcast(I32), 0).then_inc(k_zeroed, 1)
            for n, (raw, hi, lo) in enumerate(((w_raw[2], wk_h, wk_l), (w_raw[3], wv_h, wv_l),
                                               (w_raw[0], wq_h, wq_l), (w_raw[1], wo_h, wo_l))):
                if n == 2:
                    stats_unit(0, 0, 0)
                    dve.wait_ge(stats_done, 1)
                    aggregate_unit(0, 0)
                rows = C - P if n < 2 else P
                dve.wait_ge(w_hi, 2 * n + 2)
                low(lo[:, 0, :], raw[:, 0, :], hi[:, 0, :], WS, w_lo)
                low(lo[0:rows, 1, :], raw[0:rows, 1, :], hi[0:rows, 1, :], WS, w_lo)
                if n == 2:
                    normalise_unit(0, 0)
                    stats_unit(1, 1, 0)
                    dve.wait_ge(stats_done, 2)
                    aggregate_unit(1, 1)
                    xt_low(0, 0)

            def step(u, s, turn, has):
                if has(1):
                    normalise_unit(u + 1, 1 - s)
                if has(2):
                    stats_unit(u + 2, s, turn + 1)
                    dve.wait_ge(stats_done, u + 3)
                k_low(u, s, turn)
                if has(2):
                    aggregate_unit(u + 2, s)
                q_low(u, s, turn)
                if has(1):
                    xt_low(u + 1, 1 - s)

            walk(dve, step)

        @block.scalar
        def _(act):
            def xt_high(u, s):
                act.wait_ge(xt_ready, u + 1)
                if not early(u):
                    act.wait_ge(q_ready, u - 1)
                nc.scalar.activation(xt_h[s][:], ps_x[:], ACT.Copy).then_inc(xt_hi, 1)

            def k_high(u, s, turn):
                act.wait_ge(k_ready, u + 1)
                if not early(u):
                    act.wait_ge(k_stored[s], 32 * turn)
                nc.scalar.activation(k_h[s][:].rearrange("p b e t -> p e b t"),
                                     ps_k[:].rearrange("p e (b t) -> p e b t", b=2), ACT.Copy, scale=1.0 / WS).then_inc(k_hi, 1)

            def q_high(u, s, turn):
                act.wait_ge(q_ready, u + 1)
                if not early(u):
                    act.wait_ge(q_stored[s], 32 * turn)
                nc.scalar.activation(q_h[s][:].rearrange("p b e t -> p e b t"),
                                     ps_q[:].rearrange("p e (b t) -> p e b t", b=2), ACT.Copy, scale=SC / WS).then_inc(q_hi, 1)

            def v_copy(u):
                act.wait_ge(v_ready, u + 1)
                nc.scalar.activation(v_all[:, bass.ds(UT * u, UT), :].rearrange("p t n -> p (t n)"),
                                     ps_v[:].rearrange("p a b -> p (a b)"), ACT.Copy, scale=1.0 / WS).then_inc(v_copied, 1)

            for n, (raw, hi) in enumerate(((w_raw[2], wk_h), (w_raw[3], wv_h), (w_raw[0], wq_h), (w_raw[1], wo_h))):
                rows = C - P if n < 2 else P
                act.wait_ge(w_loaded, 96)
                nc.scalar.activation(hi[:, 0, :], raw[:, 0, :], ACT.Copy, scale=WS).then_inc(w_hi, 1)
                nc.scalar.activation(hi[0:rows, 1, :], raw[0:rows, 1, :], ACT.Copy, scale=WS).then_inc(w_hi, 1)
            xt_high(0, 0)

            def step(u, s, turn, has):
                k_high(u, s, turn)
                q_high(u, s, turn)
                if has(1):
                    xt_high(u + 1, 1 - s)
                v_copy(u)

            walk(act, step)

        @block.tensor
        def _(pe):
            def transpose_x(u, s, first):
                pe.wait_ge(xn_done, u + 1)
                if not first:
                    pe.wait_ge(xt_lo, u)
                for k in range(DK):
                    for t in range(UT):
                        last = nc.tensor.transpose(ps_x[:, k, P * t:P * (t + 1)], xn[s][:, t, P * k:P * (k + 1)], ident[:])
                last.then_inc(xt_ready, 1)

            def project_q(u, s, first):
                pe.wait_ge(xt_lo, u + 1)
                if not first:
                    pe.wait_ge(q_lo, 2 * u)
                for e in range(2):
                    cols = slice(P * e, P * (e + 1))
                    for n, (w, v) in enumerate(((wq_h, xt_h), (wq_l, xt_h), (wq_h, xt_l))):
                        for k in range(DK):
                            last = nc.tensor.matmul(ps_q[:, e, :], w[:, k, cols], v[s][:, k, :],
                                                    start=(n + k == 0), stop=(n == 2 and k == DK - 1))
                last.then_inc(q_ready, 1)

            def project_k(u, s, first):
                pe.wait_ge(ctx_split, 4 * u + 4)
                if not first:
                    pe.wait_ge(k_lo, 2 * u)
                for e in range(2):
                    cols = slice(P * e, P * (e + 1))
                    for n, (w, v) in enumerate(((wk_h, ctx_h), (wk_l, ctx_h), (wk_h, ctx_l))):
                        for k, rows in ((0, P), (1, C - P)):
                            last = nc.tensor.matmul(ps_k[:, e, :], w[0:rows, k, cols], v[s][0:rows, k, :],
                                                    start=(n + k == 0), stop=(n == 2 and k == DK - 1))
                last.then_inc(k_ready, 1)

            def project_v(u, s, first):
                if not first:
                    pe.wait_ge(v_copied, u)
                for t in range(UT):
                    for n, (v, w) in enumerate(((ctx_h, wv_h), (ctx_h, wv_l), (ctx_l, wv_h))):
                        for k, rows in ((0, P), (1, C - P)):
                            last = nc.tensor.matmul(ps_v[:, t // 2, D * (t % 2):D * (t % 2 + 1)],
                                                    v[s][0:rows, k, P * t:P * (t + 1)], w[0:rows, k, :],
                                                    start=(n + k == 0), stop=(n == 2 and k == DK - 1))
                last.then_inc(v_ready, 1)

            pe.wait_ge(consts_ready, 3)
            pe.wait_ge(w_lo, 6)
            transpose_x(0, 0, True)

            def step(u, s, turn, has):
                project_k(u, s, not has(-1))
                project_q(u, s, not has(-1))
                if has(1):
                    transpose_x(u + 1, 1 - s, False)
                project_v(u, s, not has(-1))

            walk(pe, step)


def attend(nc, x1, ident, bo_bc, wo_h, wo_l, q_dram, k_dram, v_all, q_stack, k_stack, v_pad,
           wg, wu, wd, w32, w16, w_large):
    stack = ExitStack()
    with stack:
        def sb(name, shape, dt):
            return stack.enter_context(nc.sbuf_tensor(name, shape, dt))

        def sem(name):
            return stack.enter_context(nc.semaphore(name))

        probs = [sb(f"probs{i}", [P, 2, 2, 2, N], F32) for i in range(2)]
        neg_max = [sb(f"neg_max{i}", [P, P], F32) for i in range(2)]
        max_t = [sb(f"max_t{i}", [2 * H, P], F16) for i in range(2)]
        o_t = sb("o_t", [P, GROUPS, N], F32)
        rsum = [sb(f"rsum{i}", [P, H], F32) for i in range(2)]
        o_n = [sb(f"o_n{i}", [P, H, HD], F32) for i in range(2)]
        ot_h = sb("ot_h", [P, DK, N], F16)
        ot_l = sb("ot_l", [P, DK, N], F16)

        ps_s = [stack.enter_context(nc.psum_tensor(f"ps_s{i}", [P, 2, 2, N], F32)) for i in range(2)]
        ps_m = [stack.enter_context(nc.psum_tensor(f"ps_m{i}", [P, 2, N], F32)) for i in range(2)]
        ps_o = stack.enter_context(nc.psum_tensor("ps_o", [P, 2 * N], F32))
        ps_c = stack.enter_context(nc.psum_tensor("ps_c", [P, 512], F32))

        w_max = sb("w_max", [P, 4], F32)
        w_top = sb("w_top", [P, 1], F32)
        w_loaded = [sem(f"w_loaded{n}") for n in range(3)]
        w_made, w_max_done, w_flag = sem("w_made"), sem("w_max_done"), sem("w_flag")
        qk_loaded = [sem(f"qk_loaded{i}") for i in range(RING)]
        max_loaded = [sem(f"max_loaded{i}") for i in range(RING)]
        max_cleared, v_padded, bo_added = sem("max_cleared"), sem("v_padded"), sem("bo_added")
        head_scored, head_reduced = sem("head_scored"), sem("head_reduced")
        max_transposed, max_copied = sem("max_transposed"), sem("max_copied")
        pair_scored, pair_exp = sem("pair_scored"), sem("pair_exp")
        pv_ready, pv_copied = sem("pv_ready"), sem("pv_copied")
        back_ready, recip_done, normed = sem("back_ready"), sem("recip_done"), sem("normed")
        ot_ready, ot_hi, ot_lo = sem("ot_ready"), sem("ot_hi"), sem("ot_lo")
        wo_ready, res_done = sem("wo_ready"), sem("res_done")

        LOOPS = 3
        QK_DMAS = 8

        def walk(eng, start, step):
            for i in range(start):
                step(i, i, lambda d: (i + d) // RING, lambda d: i + d >= 0)
            with eng.Fori(0, LOOPS) as j:
                for k in range(start, start + RING):
                    step(RING * j + k, k, lambda d: j + (k + d) // RING, lambda d: True)
            for i in range(start + LOOPS * RING, B + 1):
                step(i, i, lambda d: (i + d) // RING, lambda d: i + d < B)

        block = stack.enter_context(nc.Block())

        @block.sync
        def _(sp):
            def load_qk(b, r):
                for e in range(2):
                    def rows(a, first, n):
                        return a[r][64 * e + first:64 * e + first + n].rearrange("r p t -> r (p t)")
                    q_src = q_dram[bass.ds(b, 1), e].rearrange("b l (r p) t -> (b l r) (p t)", p=PAIRS)
                    k_src = k_dram[bass.ds(b, 1), e].rearrange("b l (r p) t -> (b l r) (p t)", p=PAIRS)
                    sp.dma_start(rows(q_stack, 0, 2 * HD), q_src).then_inc(qk_loaded[r], 16)
                    sp.dma_start(rows(q_stack, 2 * HD, HD), q_src[0:HD]).then_inc(qk_loaded[r], 16)
                    sp.dma_start(rows(k_stack, HD, 2 * HD), k_src).then_inc(qk_loaded[r], 16)
                    sp.dma_start(rows(k_stack, 0, HD), k_src[0:HD]).then_inc(qk_loaded[r], 16)

            def load_max(b, r):
                sp.wait_ge(max_copied, b + 1)
                for e in range(2):
                    sp.dma_start(q_stack[r][64 * e + ROW_MAX:64 * e + ROW_MAX + 1, :, :],
                                 max_t[r % 2][H * e:H * (e + 1), :]).then_inc(max_loaded[r], 16)

            def step(i, r, turn, has):
                if has(3) and has(-1):
                    sp.wait_ge(pair_scored, PAIRS * i)
                    load_qk(i + 3, (r + 3) % RING)
                if has(1):
                    load_max(i + 1, (r + 1) % RING)

            for b in range(3):
                load_qk(b, b)
            load_max(0, 0)
            load_qk(3, 3)
            for n, w in enumerate((wg, wu, wd)):
                sp.dma_start(w32[n][:].bitcast(I32), w.rearrange("(k p) n -> p k n", p=P)).then_inc(w_loaded[n], 16)
            walk(sp, 1, step)
            for r in range(RING):
                sp.wait_ge(qk_loaded[r], 16 * QK_DMAS * B // RING)
                sp.wait_ge(max_loaded[r], 32 * B // RING)

        @block.gpsimd
        def _(pool):
            def pad_v(b, r):
                nc.gpsimd.tensor_copy(v_pad[r][:, :, :, 0:HD],
                                      v_all[:, bass.ds(2 * b, 2), :].rearrange("p t (h d) -> p t h d", h=H)).then_inc(v_padded, 1)

            def add_bo(b):
                for t in range(2):
                    tile = x1[:, bass.ds(2 * b + t, 1), :].rearrange("p a d -> p (a d)")
                    nc.gpsimd.tensor_tensor(tile, tile, bo_bc[:], ALU.add).then_inc(bo_added, 1)

            def step(i, r, turn, has):
                if has(3) and has(-1):
                    pool.wait_ge(pv_ready, GROUPS * i)
                if has(2):
                    add_bo(i + 2)
                if has(3):
                    pad_v(i + 3, (r + 3) % RING)

            for n in range(2):
                nc.gpsimd.memset(neg_max[n][:], 0.0).then_inc(max_cleared, 1)
            for b in range(3):
                pad_v(b, b)
            for b in range(2):
                add_bo(b)
            for n in range(3):
                pool.wait_ge(w_loaded[n], 16)
                nc.gpsimd.tensor_copy(w32[n][:], w32[n][:].bitcast(I32)).then_inc(w_made, 1)
                pool.wait_ge(w_made, 2 * n + 1)
                nc.gpsimd.tensor_copy(w16[n][:], w32[n][:]).then_inc(w_made, 1)
            walk(pool, 1, step)
            pool.wait_ge(w_max_done, 4)
            nc.gpsimd.partition_all_reduce(w_top[:], w_max[:, 3:4], P, bass.bass_isa.ReduceOp.max).then_inc(w_flag, 1)
            pool.wait_ge(w_flag, 1)
            nc.gpsimd.tensor_scalar(w_large[:], w_top[:], INT_EXACT, None, ALU.is_gt).then_inc(w_flag, 1)
            pool.wait_ge(w_flag, 2)

        @block.vector
        def _(dve):
            def reduce_pair(b, r, p, first):
                for e in range(2):
                    dve.wait_ge(head_scored, H * b + 2 * p + e + 1)
                    if p == 0 and e == 0 and not first:
                        dve.wait_ge(max_transposed, b - 1)
                    col = 2 * PAIRS * e + 2 * p
                    nc.vector.tensor_reduce(neg_max[r % 2][:, col:col + 2], ps_m[e][:], AXX, ALU.max,
                                            negate=True).then_inc(head_reduced, 1)

            def normalise(b, h):
                dve.wait_ge(back_ready, 2 * b + h + 1)
                dve.wait_ge(normed, 2 * b)
                heads = ps_c[:].rearrange("p (h c) -> p h c", h=H)
                nc.vector.reciprocal(rsum[h][:], heads[:, :, HD]).then_inc(recip_done, 1)
                dve.wait_ge(recip_done, 2 * b + h + 1)
                dve.wait_ge(ot_ready, b)
                nc.vector.tensor_tensor(o_n[h][:], heads[:, :, 0:HD],
                                        rsum[h][:].unsqueeze(2).to_broadcast([P, H, HD]), ALU.mult).then_inc(normed, 1)

            def ot_low(b):
                dve.wait_ge(ot_hi, b + 1)
                nc.vector.tensor_tensor(ot_l[:].rearrange("p k t -> p (k t)"), ps_c[:],
                                        ot_h[:].rearrange("p k t -> p (k t)"), ALU.subtract).then_inc(ot_lo, 1)

            def residual(b):
                dve.wait_ge(wo_ready, b + 1)
                dve.wait_ge(bo_added, 2 * b + 2)
                tiles = x1[:, bass.ds(2 * b, 2), :].rearrange("p t d -> p (t d)")
                nc.vector.scalar_tensor_tensor(out=tiles, in0=ps_c[:], scalar=1.0 / WS, in1=tiles,
                                               op0=ALU.mult, op1=ALU.add).then_inc(res_done, 1)

            def step(i, r, turn, has):
                for p in range(PAIRS):
                    if 4 <= p < 7 and has(0) and not has(1):
                        dve.wait_ge(w_made, 2 * (p - 4) + 1)
                        w = w32[p - 4][:]
                        nc.vector.tensor_reduce(w_max[:, p - 4:p - 3], w.rearrange("p k n -> p (k n)"), AXX, ALU.max,
                                                apply_absolute_value=True).then_inc(w_max_done, 1)
                    if p == 7 and has(0) and not has(1):
                        dve.wait_ge(w_max_done, 3)
                        nc.vector.tensor_reduce(w_max[:, 3:4], w_max[:, 0:3], AXX, ALU.max).then_inc(w_max_done, 1)
                    if p < 4 and has(1):
                        reduce_pair(i + 1, (r + 1) % RING, p + 4, False)
                    if p >= 4 and has(2):
                        reduce_pair(i + 2, (r + 2) % RING, p - 4, False)
                    if has(-1):
                        if p in (1, 2):
                            normalise(i - 1, p - 1)
                        if p == 3:
                            ot_low(i - 1)
                        if p == 5:
                            residual(i - 1)

            dve.wait_ge(max_cleared, 2)
            for p in range(PAIRS):
                reduce_pair(0, 0, p, True)
            for p in range(4):
                reduce_pair(1, 1, p, True)
            walk(dve, 2, step)

        @block.scalar
        def _(act):
            def exp_pair(b, p, first):
                g = p // 2
                act.wait_ge(pair_scored, PAIRS * b + p + 1)
                if p % 2 == 0 and not (first and g < 2):
                    act.wait_ge(pv_ready, GROUPS * b + g - 1)
                nc.scalar.activation(probs[g % 2][:, p % 2].rearrange("p e k q -> p (e k q)"),
                                     ps_s[p % 2][:].rearrange("p e k q -> p (e k q)"), ACT.Exp).then_inc(pair_exp, 1)

            def copy_pv(b, g, first):
                act.wait_ge(pv_ready, GROUPS * b + g + 1)
                if g == 0 and not first:
                    act.wait_ge(back_ready, 2 * b)
                nc.scalar.activation(o_t[:, g, :], ps_o[:, 0:N], ACT.Copy).then_inc(pv_copied, 1)

            def ot_high(b, first):
                act.wait_ge(ot_ready, b + 1)
                if not first:
                    act.wait_ge(wo_ready, b)
                nc.scalar.activation(ot_h[:].rearrange("p k t -> p (k t)"), ps_c[:], ACT.Copy).then_inc(ot_hi, 1)

            def copy_max(b, r, turn):
                act.wait_ge(max_transposed, b + 1)
                if turn is not None:
                    act.wait_ge(max_loaded[(r + 2) % RING], 32 * turn)
                nc.scalar.activation(max_t[r % 2][:], ps_c[0:2 * H, 0:P], ACT.Copy).then_inc(max_copied, 1)

            def step(i, r, turn, has):
                for p in range(PAIRS):
                    if p == 0 and has(-1):
                        copy_pv(i - 1, 3, False)
                    if has(0):
                        if p in (2, 4, 6):
                            copy_pv(i, p // 2 - 1, not has(-1))
                        exp_pair(i, p, not has(-1))
                    if p == 3 and has(-1):
                        ot_high(i - 1, not has(-2))
                    if p == 4 and has(1):
                        copy_max(i + 1, (r + 1) % RING, turn(-1) + 1 if has(-1) else None)

            copy_max(0, 0, None)
            walk(act, 2, step)

        @block.tensor
        def _(pe):
            def score_for_max(b, r, turn, p, first):
                if p == 0:
                    pe.wait_ge(qk_loaded[r], 16 * QK_DMAS * (turn + 1))
                for e in range(2):
                    if not (first and p == 0):
                        pe.wait_ge(head_reduced, H * b + 2 * p + e - 1)
                    rows = slice(64 * e, 64 * e + ROW_MAX)
                    for h in range(2):
                        last = nc.tensor.matmul(ps_m[e][:, h, :], q_stack[r][rows, p, P * h:P * (h + 1)],
                                                k_stack[r][rows, p, :], start=True, stop=True)
                    last.then_inc(head_scored, 1)

            def score_pair(b, r, turn, p, first):
                if p == 0:
                    pe.wait_ge(max_loaded[r], 32 * (turn + 1))
                if not (first and p < 2):
                    pe.wait_ge(pair_exp, PAIRS * b + p - 1)
                for e in range(2):
                    rows = slice(64 * e, 64 * e + ROW_MAX + 1)
                    for k in range(2):
                        last = nc.tensor.matmul(ps_s[p % 2][:, e, k, :], k_stack[r][rows, p, P * k:P * (k + 1)],
                                                q_stack[r][rows, p, :], start=True, stop=True)
                last.then_inc(pair_scored, 1)

            def weigh_values(b, r, g, first):
                if g == 0:
                    pe.wait_ge(v_padded, b + 1)
                pe.wait_ge(pair_exp, PAIRS * b + 2 * g + 2)
                if not (first and g == 0):
                    pe.wait_ge(pv_copied, GROUPS * b + g)
                for k in range(2):
                    for h in range(4):
                        last = nc.tensor.matmul(ps_o[32 * h:32 * h + 32, 0:N], v_pad[r][:, k, 4 * g + h, :],
                                                probs[g % 2][:, h // 2, h % 2, k, :], start=(k == 0), stop=(k == 1))
                last.then_inc(pv_ready, 1)

            def transpose_max(b, r, first):
                pe.wait_ge(head_reduced, H * b + H)
                if not first:
                    pe.wait_ge(ot_lo, b - 1)
                elif b == 1:
                    pe.wait_ge(max_copied, 1)
                nc.tensor.transpose(ps_c[:, 0:P], neg_max[r % 2][:], ident[:]).then_inc(max_transposed, 1)

            def back(b, h):
                if h == 0:
                    pe.wait_ge(pv_copied, GROUPS * b + GROUPS)
                else:
                    pe.wait_ge(normed, 2 * b + 1)
                for g in range(GROUPS):
                    last = nc.tensor.transpose(ps_c[:, P * g:P * (g + 1)], o_t[:, g, P * h:P * (h + 1)], ident[:])
                last.then_inc(back_ready, 1)

            def transpose_o(b):
                pe.wait_ge(normed, 2 * b + 2)
                for k in range(DK):
                    for h in range(2):
                        last = nc.tensor.transpose(ps_c[:, N * k + P * h:N * k + P * (h + 1)],
                                                   o_n[h][:, PAIRS * k:PAIRS * (k + 1), :].rearrange("p h d -> p (h d)"), ident[:])
                last.then_inc(ot_ready, 1)

            def project_o(b, maxima):
                pe.wait_ge(ot_lo, b + 1)
                if maxima:
                    pe.wait_ge(max_copied, b + 3)
                for h in range(2):
                    for n, (o, w) in enumerate(((ot_h, wo_h), (ot_h, wo_l), (ot_l, wo_h))):
                        for k in range(DK):
                            last = nc.tensor.matmul(ps_c[:, D * h:D * (h + 1)], o[:, k, P * h:P * (h + 1)], w[:, k, :],
                                                    start=(n + k == 0), stop=(n == 2 and k == DK - 1))
                last.then_inc(wo_ready, 1)

            def step(i, r, turn, has):
                for p in range(PAIRS):
                    if p < 4 and has(1):
                        score_for_max(i + 1, (r + 1) % RING, turn(1), p + 4, False)
                    if p >= 4 and has(2):
                        score_for_max(i + 2, (r + 2) % RING, turn(2), p - 4, False)
                    if has(0):
                        score_pair(i, r % RING, turn(0), p, not has(-1))
                    if p == 0 and has(-1):
                        weigh_values(i - 1, (r - 1) % RING, 3, False)
                    if p in (1, 2) and has(-1):
                        if p == 1:
                            pe.wait_ge(res_done, i - 1)
                            if has(0):
                                pe.wait_ge(max_copied, i + 1)
                        back(i - 1, p - 1)
                    if p == 3 and has(-1):
                        transpose_o(i - 1)
                    if p == 4 and has(1):
                        transpose_max(i + 1, (r + 1) % RING, not has(-1))
                    if p == 5 and has(-1):
                        project_o(i - 1, has(1))
                    if p in (2, 4, 6) and has(0):
                        weigh_values(i, r % RING, p // 2 - 1, not has(-1))

            for p in range(PAIRS):
                score_for_max(0, 0, 0, p, True)
            for p in range(4):
                if p == 1:
                    transpose_max(0, 0, True)
                score_for_max(1, 1, 0, p, False)
            walk(pe, 2, step)


def feed(nc, out, x1, ident, half, eps, w32, w16, w_large):
    stack = ExitStack()
    with stack:
        def sb(name, shape, dt):
            return stack.enter_context(nc.sbuf_tensor("feed_" + name, shape, dt))

        def sem(name):
            return stack.enter_context(nc.semaphore("feed_" + name))

        stats = [sb(f"stats{i}", [P, UT, 6], F32) for i in range(2)]
        mean_var = [sb(f"mean_var{i}", [P, UT, 2], F32) for i in range(2)]
        rstd = [sb(f"rstd{i}", [P, UT], F32) for i in range(2)]
        var_eps = sb("var_eps", [P, UT], F32)
        xn = [sb(f"xn{i}", [P, UT, D], F32) for i in range(2)]
        xt_f = [sb(f"xt_f{i}", [P, DK, U], F32) for i in range(2)]
        xt_h = [sb(f"xt_h{i}", [P, DK, U], F16) for i in range(2)]
        xt_l = [sb(f"xt_l{i}", [P, DK, U], F16) for i in range(2)]
        silu = [sb(f"silu{i}", [P, U], F32) for i in range(2)]
        hid_f = [sb(f"hid_f{i}", [P, FT, U], F32) for i in range(2)]
        hid_h = [sb(f"hid_h{i}", [P, FT, U], F16) for i in range(2)]
        hid_l = [sb(f"hid_l{i}", [P, FT, U], F16) for i in range(2)]

        ps_x = stack.enter_context(nc.psum_tensor("feed_ps_x", [P, DK, U], F32))
        ps_g = [stack.enter_context(nc.psum_tensor(f"ps_g{i}", [P, U], F32)) for i in range(2)]
        ps_u = [stack.enter_context(nc.psum_tensor(f"ps_u{i}", [P, U], F32)) for i in range(2)]
        ps_y = stack.enter_context(nc.psum_tensor("ps_y", [P, UT, D], F32))

        stats_done, mv_done, var_done, rstd_done, xn_done = (sem(n) for n in (
            "stats_done", "mv_done", "var_done", "rstd_done", "xn_done"))
        xt_ready, xt_full, xt_hi, xt_lo = sem("xt_ready"), sem("xt_full"), sem("xt_hi"), sem("xt_lo")
        gu_ready, silu_done, hid_done, hid_hi, hid_lo = (sem(n) for n in (
            "gu_ready", "silu_done", "hid_done", "hid_hi", "hid_lo"))
        y_ready, y_done = sem("y_ready"), sem("y_done")
        stored = [sem(f"stored{i}") for i in range(2)]

        def walk(eng, step):
            for u in range(2):
                step(u, u % 2, lambda d: u + d >= 0)
            with eng.Fori(1, NU // 2 - 1) as j:
                for s in range(2):
                    step(2 * j + s, s, lambda d: True)
            for u in range(NU - 2, NU):
                step(u, u % 2, lambda d: u + d < NU)

        block = stack.enter_context(nc.Block())

        @block.sync
        def _(sp):
            def step(u, s, has):
                sp.wait_ge(y_done, u + 1)
                sp.dma_start(out[bass.ds(U * u, U), :].rearrange("(t p) d -> p t d", p=P),
                             x1[:, bass.ds(UT * u, UT), :]).then_inc(stored[s], 16)

            walk(sp, step)
            for s in range(2):
                sp.wait_ge(stored[s], 16 * NU // 2)

        @block.gpsimd
        def _(pool):
            def rstd_unit(u, s):
                pool.wait_ge(mv_done, u + 1)
                nc.gpsimd.tensor_tensor(var_eps[:], mean_var[s][:, :, 1], eps[:], ALU.add).then_inc(var_done, 1)
                pool.wait_ge(var_done, u + 1)
                nc.gpsimd.tensor_tensor(rstd[s][:], var_eps[:], half[:], ALU.pow).then_inc(rstd_done, 1)
                pool.wait_ge(rstd_done, u + 1)

            def step(u, s, has):
                if has(2):
                    rstd_unit(u + 2, s)

            rstd_unit(0, 0)
            rstd_unit(1, 1)
            walk(pool, step)

        @block.vector
        def _(dve):
            def stats_unit(u, s, first):
                if not first:
                    dve.wait_ge(mv_done, u - 1)
                    dve.wait_ge(xn_done, u - 1)
                    dve.wait_ge(rstd_done, u - 1)
                for t in range(UT):
                    last = nc.vector.bn_stats(stats[s][:, t, :], x1[:, bass.ds(UT * u + t, 1), :].rearrange("p a d -> p (a d)"))
                last.then_inc(stats_done, 1)

            def aggregate_unit(u, s):
                for t in range(UT):
                    last = nc.vector.bn_aggr(mean_var[s][:, t, :], stats[s][:, t, :])
                last.then_inc(mv_done, 1)

            def normalise_unit(u, s, first):
                dve.wait_ge(rstd_done, u + 1)
                if not first:
                    dve.wait_ge(xt_ready, u - 1)
                for t in range(UT):
                    last = nc.vector.tensor_scalar(xn[s][:, t, :], x1[:, bass.ds(UT * u + t, 1), :].rearrange("p a d -> p (a d)"),
                                                   mean_var[s][:, t, 0:1], rstd[s][:, t:t + 1],
                                                   ALU.subtract, ALU.mult)
                last.then_inc(xn_done, 1)

            def xt_low(u, s):
                dve.wait_ge(xt_hi, u + 1)
                nc.vector.tensor_tensor(xt_l[s][:], ps_x[:], xt_h[s][:], ALU.subtract).then_inc(xt_lo, 1)

            def hidden(u, s, f, first):
                dve.wait_ge(silu_done, FT * u + f + 1)
                if f == 0 and not first:
                    dve.wait_ge(y_ready, u - 1)
                    dve.wait_ge(hid_hi, FT * (u - 1))
                nc.vector.scalar_tensor_tensor(out=hid_f[s][:, f, :], in0=ps_u[f % 2][:], scalar=W_SCALE * HS,
                                               in1=silu[f % 2][:], op0=ALU.mult, op1=ALU.mult).then_inc(hid_done, 1)

            def hidden_low(u, s, f):
                dve.wait_ge(hid_hi, FT * u + f + 1)
                nc.vector.tensor_tensor(hid_l[s][:, f, :], hid_f[s][:, f, :], hid_h[s][:, f, :],
                                        ALU.subtract).then_inc(hid_lo, 1)

            def residual(u):
                dve.wait_ge(y_ready, u + 1)
                tiles = x1[:, bass.ds(UT * u, UT), :].rearrange("p t d -> p (t d)")
                nc.vector.scalar_tensor_tensor(out=tiles, in0=ps_y[:].rearrange("p t d -> p (t d)"),
                                               scalar=W_SCALE / HS, in1=tiles,
                                               op0=ALU.mult, op1=ALU.add).then_inc(y_done, 1)

            def step(u, s, has):
                for f in range(FT):
                    hidden(u, s, f, not has(-2))
                    if f == 0 and has(1):
                        normalise_unit(u + 1, 1 - s, not has(-1))
                    if f > 0:
                        hidden_low(u, s, f - 1)
                    if f == 3:
                        if has(1):
                            xt_low(u + 1, 1 - s)
                        if has(2):
                            stats_unit(u + 2, s, False)
                            dve.wait_ge(stats_done, u + 3)
                        if has(-1):
                            residual(u - 1)
                        if has(2):
                            aggregate_unit(u + 2, s)
                hidden_low(u, s, FT - 1)

            for u in range(2):
                stats_unit(u, u, True)
                dve.wait_ge(stats_done, u + 1)
                aggregate_unit(u, u)
            normalise_unit(0, 0, True)
            xt_low(0, 0)
            walk(dve, step)
            residual(NU - 1)

        @block.scalar
        def _(act):
            def xt_copy(u, s, first):
                act.wait_ge(xt_ready, u + 1)
                if not first:
                    act.wait_ge(gu_ready, FT * (u - 1))
                nc.scalar.activation(xt_f[s][:], ps_x[:], ACT.Copy).then_inc(xt_full, 1)
                nc.scalar.activation(xt_h[s][:], ps_x[:], ACT.Copy).then_inc(xt_hi, 1)

            def gate_silu(u, f, first):
                act.wait_ge(gu_ready, FT * u + f + 1)
                if not (first and f < 2):
                    act.wait_ge(hid_done, FT * u + f - 1)
                nc.scalar.activation(silu[f % 2][:], ps_g[f % 2][:], ACT.Silu, scale=W_SCALE).then_inc(silu_done, 1)

            def hidden_high(u, s, f, first):
                act.wait_ge(hid_done, FT * u + f + 1)
                if f == 0 and not first:
                    act.wait_ge(y_ready, u - 1)
                    act.wait_ge(hid_lo, FT * (u - 1))
                nc.scalar.activation(hid_h[s][:, f, :], hid_f[s][:, f, :], ACT.Copy).then_inc(hid_hi, 1)

            def step(u, s, has):
                for f in range(FT):
                    gate_silu(u, f, not has(-1))
                    if f > 0:
                        hidden_high(u, s, f - 1, not has(-2))
                    if f == 2 and has(1):
                        xt_copy(u + 1, 1 - s, not has(-1))
                hidden_high(u, s, FT - 1, False)

            xt_copy(0, 0, True)
            walk(act, step)

        @block.tensor
        def _(pe):
            def transpose_x(u, s, first):
                pe.wait_ge(xn_done, u + 1)
                if not first:
                    pe.wait_ge(xt_lo, u)
                for k in range(DK):
                    for t in range(UT):
                        last = nc.tensor.transpose(ps_x[:, k, P * t:P * (t + 1)], xn[s][:, t, P * k:P * (k + 1)], ident[:])
                last.then_inc(xt_ready, 1)

            def gate_up(u, s, f, first, split):
                if f == 0:
                    pe.wait_ge(xt_lo, u + 1)
                if not (first and f < 2):
                    pe.wait_ge(hid_done, FT * u + f - 1)
                for n, ps in ((0, ps_g), (1, ps_u)):
                    terms = [(w16[n], xt_h[s]), (w16[n], xt_l[s])] if split else [(w32[n], xt_f[s])]
                    for m, (w, v) in enumerate(terms):
                        for k in range(DK):
                            last = nc.tensor.matmul(ps[f % 2][:], w[:, k, P * f:P * (f + 1)], v[:, k, :],
                                                    start=(m + k == 0), stop=(m == len(terms) - 1 and k == DK - 1))
                last.then_inc(gu_ready, 1)

            def down(u, s, first, split):
                pe.wait_ge(hid_lo, FT * u + FT)
                if not first:
                    pe.wait_ge(y_done, u)
                terms = [(hid_h[s], w16[2]), (hid_l[s], w16[2])] if split else [(hid_f[s], w32[2])]
                for t in range(UT):
                    for m, (v, w) in enumerate(terms):
                        for f in range(FT):
                            last = nc.tensor.matmul(ps_y[:, t, :], v[:, f, P * t:P * (t + 1)], w[:, f, :],
                                                    start=(m + f == 0), stop=(m == len(terms) - 1 and f == FT - 1))
                last.then_inc(y_ready, 1)

            def whole(split):
                def step(u, s, has):
                    for f in range(FT):
                        gate_up(u, s, f, not has(-1), split)
                        if f == 2 and has(1):
                            transpose_x(u + 1, 1 - s, False)
                        if f == 3 and has(-1):
                            down(u - 1, 1 - s, not has(-2), split)

                transpose_x(0, 0, True)
                walk(pe, step)
                down(NU - 1, 1, False, split)

            large = pe.value_load(w_large[0:1, 0:1], min_val=0, max_val=1)
            with pe.If(large == 0):
                whole(True)
            with pe.Else():
                whole(False)


def kernel(**inputs):
    import numpy as _np
    import concourse.bacc as _bacc
    from concourse import mybir as _mybir
    from concourse.bass_utils import run_bass_kernel_spmd as _run

    def by_row(w):
        return _np.asarray(w).reshape(-1, PAIRS, 2, HD).transpose(0, 2, 3, 1).reshape(-1, H * HD)

    arrays = {
        "x": _np.asarray(inputs["x"]).reshape(B * N, D),
        "ctx_t": _np.asarray(inputs["ctx_768"]).transpose(0, 2, 1),
        "wq": by_row(inputs["L0_xattn_Wq"]),
        "wk": by_row(inputs["L0_xattn_Wk"]),
        "wv": inputs["L0_xattn_Wv"],
        "wo": inputs["L0_xattn_Wo"],
        "bo": inputs["L0_xattn_bo"],
        "wg": _np.asarray(inputs["L0_ffn_w_gate"]).T,
        "wu": _np.asarray(inputs["L0_ffn_w_up"]).T,
        "wd": _np.asarray(inputs["L0_ffn_w_down"]).T,
    }
    arrays = {f"in_{k}": _np.ascontiguousarray(v) for k, v in arrays.items()}
    nc = _bacc.Bacc("TRN2", target_bir_lowering=False, num_devices=1)
    args = [nc.dram_tensor(k, a.shape, _mybir.dt.from_np(a.dtype), kind="ExternalInput").ap()
            for k, a in arrays.items()]
    out = nc.dram_tensor("out_0_dram", (B * N, D), _mybir.dt.float32, kind="ExternalOutput").ap()
    block_program(nc, *args, out)
    r = _run(nc, [arrays], core_ids=[0])
    return r.results[0]["out_0_dram"].reshape(B, N, D)
```

```python
import concourse.bass as bass
from concourse import mybir
from contextlib import ExitStack

F32 = mybir.dt.float32
F16 = mybir.dt.float16
I32 = mybir.dt.int32
ALU = mybir.AluOpType
ACT = mybir.ActivationFunctionType
AXX = mybir.AxisListType.X

B, N, D = 16, 256, 256
C = 192
H, HD = 16, 16
FF = 768
P = 128
PAIRS = H // 2
GROUPS = H // 4
U = 512
NU = B * N // U
UT = U // P
TILES = B * N // P
DK = D // P
FT = FF // P
EPS = 1e-5
WS = 16.0
SC = float(HD) ** -0.5
HS = 1.0 / 16.0
W_SCALE = 1.0 / 127.0
INT_EXACT = 2048.0
ROW_MAX = 126
RING = 4
QK_DMAS = 8


def early(u):
    return isinstance(u, int) and u < 2


def block_program(nc, x, ctx_t, wq, wk, wv, wo, bo, wg, wu, wd, out):
    stack = ExitStack()
    with stack:
        def sb(name, shape, dt, where=stack):
            return where.enter_context(nc.sbuf_tensor(name, shape, dt))

        def sem(name, where=stack):
            return where.enter_context(nc.semaphore(name))

        x1 = sb("x1", [P, TILES, D], F32)
        ident = sb("ident", [P, P], F32)
        half = sb("half", [P, UT], F32)
        eps = sb("eps", [P, UT], F32)
        bo_bc = sb("bo_bc", [P, D], F32)
        wo_h = sb("wo_h", [P, DK, D], F16)
        wo_l = sb("wo_l", [P, DK, D], F16)
        q_dram = nc.dram_tensor("q_split", (B, 2, 2, P, N), F16, kind="Internal").ap()
        k_dram = nc.dram_tensor("k_split", (B, 2, 2, P, N), F16, kind="Internal").ap()

        shapes = ([P, DK, FF], [P, DK, FF], [P, FT, D])
        w16 = [sb(f"w16_{n}", shape, F16) for n, shape in enumerate(shapes)]
        w_large = sb("w_large", [P, 1], I32)
        v_all = sb("v_all", [P, TILES, D], F32)
        q_stack = [sb(f"q_stack{i}", [P, PAIRS, N], F16) for i in range(RING)]
        k_stack = [sb(f"k_stack{i}", [P, PAIRS, 2, N], F16) for i in range(RING)]
        v_pad = [sb(f"v_pad{i}", [P, 2, H, 32], F32) for i in range(RING)]

        stats = [sb(f"stats{i}", [P, UT, 6], F32) for i in range(2)]
        mean_var = [sb(f"mean_var{i}", [P, UT, 2], F32) for i in range(2)]
        rstd = [sb(f"rstd{i}", [P, UT], F32) for i in range(2)]
        var_eps = sb("var_eps", [P, UT], F32)
        xn = [sb(f"xn{i}", [P, UT, D], F32) for i in range(2)]
        xt_h = [sb(f"xt_h{i}", [P, DK, U], F16) for i in range(2)]
        xt_l = [sb(f"xt_l{i}", [P, DK, U], F16) for i in range(2)]
        norm_buffers = (stats, mean_var, rstd, var_eps, xn, xt_h, xt_l)
        late = sb("late", [P, 3 * FT * U], F16)
        w_split = [late[:, DK * D * i:DK * D * (i + 1)].rearrange("p (k n) -> p k n", k=DK) for i in range(6)]
        rest = late[:, 6 * DK * D:]
        ctx_odd = [rest[:, DK * U * i:DK * U * (i + 1)].rearrange("p (k t) -> p k t", k=DK) for i in range(2)]
        qk_odd = [rest[:, DK * U * (i + 2):DK * U * (i + 3)].rearrange("p (b e t) -> p b e t", b=2, e=2)
                  for i in range(4)]
        q_stored = [sem(f"q_stored{i}") for i in range(2)]
        k_stored = [sem(f"k_stored{i}") for i in range(2)]
        qk_loaded = [sem(f"qk_loaded{i}") for i in range(RING)]

        project(nc, x, ctx_t, wq, wk, wv, wo, bo, x1, ident, half, eps, bo_bc, wo_h, wo_l, q_dram, k_dram,
                v_all, q_stack, k_stack, v_pad, norm_buffers, w_split, ctx_odd, qk_odd, q_stored, k_stored,
                qk_loaded)
        attend_and_feed(nc, x1, ident, bo_bc, wo_h, wo_l, q_dram, k_dram, v_all, q_stack, k_stack, v_pad,
                        wg, wu, wd, w16, w_large, out, half, eps, norm_buffers, late, w_split, ctx_odd,
                        qk_odd, q_stored, k_stored, qk_loaded)


def load_qk(sp, b, r, q_dram, k_dram, q_stack, k_stack, qk_loaded):
    for e in range(2):
        def rows(a, first, n):
            return a[64 * e + first:64 * e + first + n]
        q_place, k_place = q_stack[r][:], k_stack[r][:, :, e, :]
        q_src = q_dram[bass.ds(b, 1), e].rearrange("b l (r p) t -> (b l r) p t", p=PAIRS)
        k_src = k_dram[bass.ds(b, 1), e].rearrange("b l (r p) t -> (b l r) p t", p=PAIRS)
        sp.dma_start(rows(q_place, 0, 2 * HD), q_src).then_inc(qk_loaded[r], 16)
        sp.dma_start(rows(q_place, 2 * HD, HD), q_src[0:HD]).then_inc(qk_loaded[r], 16)
        sp.dma_start(rows(k_place, HD, 2 * HD), k_src).then_inc(qk_loaded[r], 16)
        sp.dma_start(rows(k_place, 0, HD), k_src[0:HD]).then_inc(qk_loaded[r], 16)


def project(nc, x, ctx_t, wq, wk, wv, wo, bo, x1, ident, half, eps, bo_bc, wo_h, wo_l, q_dram, k_dram,
            v_all, q_stack, k_stack, v_pad, norm_buffers, w_split, ctx_odd, qk_odd, q_stored, k_stored, qk_loaded):
    stack = ExitStack()
    with stack:
        def sb(name, shape, dt):
            return stack.enter_context(nc.sbuf_tensor(name, shape, dt))

        def sem(name):
            return stack.enter_context(nc.semaphore(name))

        w_raw = [sb(f"w_raw{i}", [P, DK, D], F32) for i in range(4)]
        wq_h, wq_l, wk_h, wk_l, wv_h, wv_l = w_split
        ctx_raw = [sb(f"ctx_raw{i}", [P, DK, U], F32) for i in range(2)]
        ctx_h = [sb("ctx_h0", [P, DK, U], F16)[:], ctx_odd[0]]
        ctx_l = [sb("ctx_l0", [P, DK, U], F16)[:], ctx_odd[1]]
        stats, mean_var, rstd, var_eps, xn, xt_h, xt_l = norm_buffers
        q_h, q_l, k_h, k_l = ([sb(f"{n}0", [P, 2, 2, N], F16)[:], odd]
                              for n, odd in zip(("q_h", "q_l", "k_h", "k_l"), qk_odd))
        diag = sb("diag", [2, 2, N], F16)

        ps_x = stack.enter_context(nc.psum_tensor("ps_x", [P, DK, U], F32))
        ps_q = stack.enter_context(nc.psum_tensor("ps_q", [P, 2, U], F32))
        ps_k = stack.enter_context(nc.psum_tensor("ps_k", [P, 2, U], F32))
        ps_v = stack.enter_context(nc.psum_tensor("ps_v", [P, 2, U], F32))

        w_loaded = [sem(f"w_loaded_{n}") for n in ("k", "v", "q", "o")]
        bo_loaded = sem("bo_loaded")
        x_loaded = [sem(f"x_loaded{i}") for i in range(2)]
        ctx_loaded = [sem(f"ctx_loaded{i}") for i in range(2)]
        q_zeroed = sem("q_zeroed")
        consts_ready = sem("consts_ready")
        ident_zero = sem("ident_zero")
        w_hi, w_lo = sem("w_hi"), sem("w_lo")
        stats_done, mv_done, var_done, rstd_done, xn_done = (sem(n) for n in (
            "stats_done", "mv_done", "var_done", "rstd_done", "xn_done"))
        first_ctx_hi, first_ctx_lo, ctx_split = sem("first_ctx_hi"), sem("first_ctx_lo"), sem("ctx_split")
        diag_made, k_zeroed, ones_loaded = sem("diag_made"), sem("k_zeroed"), sem("ones_loaded")
        xt_ready, xt_hi, xt_lo = sem("xt_ready"), sem("xt_hi"), sem("xt_lo")
        q_ready, q_hi, q_lo = sem("q_ready"), sem("q_hi"), sem("q_lo")
        k_ready, k_hi, k_lo = sem("k_ready"), sem("k_hi"), sem("k_lo")
        v_ready, v_copied = sem("v_ready"), sem("v_copied")

        def walk(eng, step):
            for u in range(2):
                step(u, u, 0, lambda d: u + d >= 0)
            with eng.Fori(1, NU // 2 - 1) as j:
                for s in range(2):
                    step(2 * j + s, s, j, lambda d: True)
            for u in range(NU - 2, NU - 1):
                step(u, u % 2, u // 2, lambda d: u + d < NU)

        block = stack.enter_context(nc.Block())

        @block.sync
        def _(sp):
            def load_unit(u, s):
                sp.dma_start(x1[:, bass.ds(UT * u, UT), :],
                             x[bass.ds(U * u, U), :].rearrange("(t p) d -> p t d", p=P)).then_inc(x_loaded[s], 16)

            def load_ctx(u, s):
                src = ctx_t[bass.ds(2 * u, 2), :, :].rearrange("b c t -> c b t")
                sp.dma_start(ctx_raw[s][:, 0, :].rearrange("c (b t) -> c b t", b=2),
                             src[0:P]).then_inc(ctx_loaded[s], 16)
                sp.dma_start(ctx_raw[s][0:C - P, 1, :].rearrange("c (b t) -> c b t", b=2),
                             src[P:C]).then_inc(ctx_loaded[s], 16)

            def store_unit(u, s):
                sp.wait_ge(k_hi, u + 1)
                sp.dma_start(k_dram[bass.ds(2 * u, 2), :, 0].rearrange("b e p t -> p (b e) t"),
                             k_h[s].rearrange("p b e t -> p (b e) t")).then_inc(k_stored[s], 16)
                sp.wait_ge(k_lo, 2 * u + 2)
                sp.dma_start(k_dram[bass.ds(2 * u, 2), :, 1].rearrange("b e p t -> p (b e) t"),
                             k_l[s].rearrange("p b e t -> p (b e) t")).then_inc(k_stored[s], 16)
                sp.wait_ge(q_hi, u + 1)
                sp.dma_start(q_dram[bass.ds(2 * u, 2), :, 0].rearrange("b e p t -> p (b e) t"),
                             q_h[s].rearrange("p b e t -> p (b e) t")).then_inc(q_stored[s], 16)
                sp.wait_ge(q_lo, 2 * u + 2)
                sp.dma_start(q_dram[bass.ds(2 * u, 2), :, 1].rearrange("b e p t -> p (b e) t"),
                             q_l[s].rearrange("p b e t -> p (b e) t")).then_inc(q_stored[s], 16)

            def load_kv_weight(n, raw, src):
                sp.dma_start(raw[:, 0, :], src[0:P, :]).then_inc(w_loaded[n], 16)
                sp.dma_start(raw[0:C - P, 1, :], src[P:C, :]).then_inc(w_loaded[n], 16)

            load_ctx(0, 0)
            load_kv_weight(0, w_raw[2], wk)
            load_unit(0, 0)
            load_kv_weight(1, w_raw[3], wv)
            sp.dma_start(w_raw[0][:], wq.rearrange("(k p) n -> p k n", p=P)).then_inc(w_loaded[2], 16)
            load_ctx(1, 1)
            load_unit(1, 1)
            sp.dma_start(w_raw[1][:], wo.rearrange("(k p) n -> p k n", p=P)).then_inc(w_loaded[3], 16)
            sp.dma_start(bo_bc[:], bo.partition_broadcast(P)).then_inc(bo_loaded, 16)

            def step(u, s, turn, has):
                if has(2):
                    sp.wait_ge(x_loaded[s], 16 * turn + 16)
                    load_unit(u + 2, s)
                    if isinstance(u, int) and u == 0:
                        sp.wait_ge(first_ctx_lo, 2)
                    else:
                        sp.wait_ge(ctx_split, 4 * u)
                    load_ctx(u + 2, s)
                if not has(2):
                    sp.wait_ge(k_stored[0], 32)
                    sp.wait_ge(q_stored[0], 32)
                    sp.wait_ge(q_zeroed, 1)
                    load_qk(sp, 0, 0, q_dram, k_dram, q_stack, k_stack, qk_loaded)
                store_unit(u, s)

            walk(sp, step)
            sp.wait_ge(bo_loaded, 16)
            sp.wait_ge(ones_loaded, 16 * RING)

        @block.gpsimd
        def _(pool):
            nc.gpsimd.memset(ident[:], 0.0).then_inc(ident_zero, 1)
            pool.wait_ge(ident_zero, 1)
            nc.gpsimd.affine_select(out=ident[:], in_=ident[:], compare_op=ALU.not_equal, fill=1.0, base=0,
                                    pattern=[[-1, P]], channel_multiplier=1).then_inc(consts_ready, 1)
            nc.gpsimd.memset(half[:], -0.5).then_inc(consts_ready, 1)
            nc.gpsimd.memset(eps[:], EPS).then_inc(consts_ready, 1)
            pool.wait_ge(consts_ready, 3)

            for r in range(RING):
                nc.gpsimd.memset(v_pad[r][:, :, :, HD:HD + 1], 1.0)
                nc.gpsimd.memset(v_pad[r][:, :, :, HD + 1:32], 0.0)

            def rstd_unit(u, s):
                pool.wait_ge(mv_done, u + 1)
                if not (isinstance(u, int) and u == 0):
                    pool.wait_ge(rstd_done, u)
                nc.gpsimd.tensor_tensor(var_eps[:], mean_var[s][:, :, 1], eps[:], ALU.add).then_inc(var_done, 1)
                pool.wait_ge(var_done, u + 1)
                nc.gpsimd.tensor_tensor(rstd[s][:], var_eps[:], half[:], ALU.pow).then_inc(rstd_done, 1)

            def split_ctx(u, s):
                for k, rows in ((0, P), (1, C - P)):
                    nc.gpsimd.tensor_copy(ctx_h[s][0:rows, k, :], ctx_raw[s][0:rows, k, :]).then_inc(ctx_split, 1)
                    pool.wait_ge(ctx_split, 4 * (u - 1) + 2 * k + 1)
                    nc.gpsimd.tensor_tensor(ctx_l[s][0:rows, k, :], ctx_raw[s][0:rows, k, :],
                                            ctx_h[s][0:rows, k, :], ALU.subtract).then_inc(ctx_split, 1)

            rstd_unit(0, 0)
            pool.wait_ge(ctx_loaded[1], 32)
            split_ctx(1, 1)
            rstd_unit(1, 1)

            def step(u, s, turn, has):
                if has(2):
                    pool.wait_ge(ctx_loaded[s], 32 * turn + 64)
                    pool.wait_ge(v_ready, u + 1)
                    rstd_unit(u + 2, s)
                    split_ctx(u + 2, s)
                if not has(-2):
                    for r in range(2 * u, 2 * u + 2):
                        nc.gpsimd.memset(q_stack[r][:].rearrange("p a t -> p (a t)").bitcast(I32), 0).then_inc(q_zeroed, 1)

            walk(pool, step)

        @block.vector
        def _(dve):
            def stats_unit(u, s, turn):
                dve.wait_ge(x_loaded[s], 16 * (turn + 1))
                if not early(u):
                    dve.wait_ge(mv_done, u - 1)
                    dve.wait_ge(xn_done, u - 1)
                    dve.wait_ge(rstd_done, u - 1)
                for t in range(UT):
                    last = nc.vector.bn_stats(stats[s][:, t, :], x1[:, bass.ds(UT * u + t, 1), :].rearrange("p a d -> p (a d)"))
                last.then_inc(stats_done, 1)

            def aggregate_unit(u, s):
                for t in range(UT):
                    last = nc.vector.bn_aggr(mean_var[s][:, t, :], stats[s][:, t, :])
                last.then_inc(mv_done, 1)

            def normalise_unit(u, s):
                dve.wait_ge(rstd_done, u + 1)
                if not early(u):
                    dve.wait_ge(xt_ready, u - 1)
                for t in range(UT):
                    last = nc.vector.tensor_scalar(xn[s][:, t, :], x1[:, bass.ds(UT * u + t, 1), :].rearrange("p a d -> p (a d)"),
                                                   mean_var[s][:, t, 0:1], rstd[s][:, t:t + 1],
                                                   ALU.subtract, ALU.mult)
                last.then_inc(xn_done, 1)

            def low(dst, ps, hi, scale, done):
                nc.vector.scalar_tensor_tensor(out=dst, in0=ps, scalar=scale, in1=hi,
                                               op0=ALU.mult, op1=ALU.subtract).then_inc(done, 1)

            def xt_low(u, s):
                dve.wait_ge(xt_hi, u + 1)
                low(xt_l[s][:], ps_x[:], xt_h[s][:], 1.0, xt_lo)

            def k_low(u, s, turn):
                dve.wait_ge(k_hi, u + 1)
                if not early(u):
                    dve.wait_ge(k_stored[s], 32 * turn)
                for e in range(2):
                    low(k_l[s][:, :, e], ps_k[:, e].rearrange("p (b t) -> p b t", b=2), k_h[s][:, :, e], 1.0 / WS, k_lo)

            def q_low(u, s, turn):
                dve.wait_ge(q_hi, u + 1)
                if not early(u):
                    dve.wait_ge(q_stored[s], 32 * turn)
                for e in range(2):
                    low(q_l[s][:, :, e], ps_q[:, e].rearrange("p (b t) -> p b t", b=2), q_h[s][:, :, e], SC / WS, q_lo)

            def weight_low(n):
                raw, hi, lo, rows = ((w_raw[2], wk_h, wk_l, C - P), (w_raw[3], wv_h, wv_l, C - P),
                                     (w_raw[0], wq_h, wq_l, P), (w_raw[1], wo_h, wo_l, P))[n]
                dve.wait_ge(w_hi, 2 * n + 2)
                low(lo[:, 0, :], raw[:, 0, :], hi[:, 0, :], WS, w_lo)
                low(lo[0:rows, 1, :], raw[0:rows, 1, :], hi[0:rows, 1, :], WS, w_lo)

            for k, rows in ((0, P), (1, C - P)):
                dve.wait_ge(first_ctx_hi, k + 1)
                nc.vector.tensor_tensor(ctx_l[0][0:rows, k, :], ctx_raw[0][0:rows, k, :], ctx_h[0][0:rows, k, :],
                                        ALU.subtract).then_inc(first_ctx_lo, 1)
            weight_low(0)
            stats_unit(0, 0, 0)
            dve.wait_ge(stats_done, 1)
            aggregate_unit(0, 0)
            weight_low(1)
            weight_low(2)
            normalise_unit(0, 0)
            stats_unit(1, 1, 0)
            dve.wait_ge(stats_done, 2)
            aggregate_unit(1, 1)

            def first_step():
                k_low(0, 0, 0)
                xt_low(0, 0)
                stats_unit(2, 0, 1)
                dve.wait_ge(stats_done, 3)
                normalise_unit(1, 1)
                aggregate_unit(2, 0)
                q_low(0, 0, 0)
                xt_low(1, 1)
                weight_low(3)

            def step(u, s, turn, has):
                if not has(-1):
                    first_step()
                    return
                if has(1):
                    normalise_unit(u + 1, 1 - s)
                if has(2):
                    stats_unit(u + 2, s, turn + 1)
                    dve.wait_ge(stats_done, u + 3)
                k_low(u, s, turn)
                if has(2):
                    aggregate_unit(u + 2, s)
                q_low(u, s, turn)
                if has(1):
                    xt_low(u + 1, 1 - s)
                if not has(-2):
                    dve.wait_ge(consts_ready, 3)
                    nc.vector.tensor_copy(diag[:], ident[0:2, 0:2].unsqueeze(2).to_broadcast([2, 2, N])).then_inc(diag_made, 1)

            walk(dve, step)

        @block.scalar
        def _(act):
            def xt_high(u, s):
                act.wait_ge(xt_ready, u + 1)
                if not early(u):
                    act.wait_ge(q_ready, u - 1)
                nc.scalar.activation(xt_h[s][:], ps_x[:], ACT.Copy).then_inc(xt_hi, 1)

            def k_high(u, s, turn):
                act.wait_ge(k_ready, u + 1)
                if not early(u):
                    act.wait_ge(k_stored[s], 32 * turn)
                nc.scalar.activation(k_h[s].rearrange("p b e t -> p e b t"),
                                     ps_k[:].rearrange("p e (b t) -> p e b t", b=2), ACT.Copy, scale=1.0 / WS).then_inc(k_hi, 1)

            def q_high(u, s, turn):
                act.wait_ge(q_ready, u + 1)
                if not early(u):
                    act.wait_ge(q_stored[s], 32 * turn)
                nc.scalar.activation(q_h[s].rearrange("p b e t -> p e b t"),
                                     ps_q[:].rearrange("p e (b t) -> p e b t", b=2), ACT.Copy, scale=SC / WS).then_inc(q_hi, 1)

            def v_copy(u):
                act.wait_ge(v_ready, u + 1)
                nc.scalar.activation(v_all[:, bass.ds(UT * u, UT), :].rearrange("p t n -> p (t n)"),
                                     ps_v[:].rearrange("p a b -> p (a b)"), ACT.Copy, scale=1.0 / WS).then_inc(v_copied, 1)

            def weight_high(n):
                raw, hi, rows = ((w_raw[2], wk_h, C - P), (w_raw[3], wv_h, C - P), (w_raw[0], wq_h, P), (w_raw[1], wo_h, P))[n]
                act.wait_ge(w_loaded[n], 32 if n < 2 else 16)
                nc.scalar.activation(hi[:, 0, :], raw[:, 0, :], ACT.Copy, scale=WS).then_inc(w_hi, 1)
                nc.scalar.activation(hi[0:rows, 1, :], raw[0:rows, 1, :], ACT.Copy, scale=WS).then_inc(w_hi, 1)

            def zero_k(r):
                nc.scalar.activation(k_stack[r][:].rearrange("p a e t -> p (a e t)").bitcast(F32),
                                     ident[:, 0:1].to_broadcast([P, PAIRS * N]), ACT.Copy, scale=0.0).then_inc(k_zeroed, 1)

            act.wait_ge(consts_ready, 3)
            zero_k(0)
            act.wait_ge(ctx_loaded[0], 32)
            for k, rows in ((0, P), (1, C - P)):
                nc.scalar.activation(ctx_h[0][0:rows, k, :], ctx_raw[0][0:rows, k, :], ACT.Copy).then_inc(first_ctx_hi, 1)
            for n in range(3):
                weight_high(n)

            def step(u, s, turn, has):
                k_high(u, s, turn)
                if not has(-1):
                    xt_high(0, 0)
                    v_copy(0)
                q_high(u, s, turn)
                if has(1):
                    xt_high(u + 1, 1 - s)
                if has(-1):
                    v_copy(u)
                else:
                    weight_high(3)
                if not has(-2):
                    for r in ((1,), (2, 3))[u]:
                        zero_k(r)
                if has(-1) and not has(-2):
                    act.wait_ge(diag_made, 1)
                    act.wait_ge(k_zeroed, RING)
                    for r in range(RING):
                        act.dma_start(k_stack[r][ROW_MAX:ROW_MAX + 2].rearrange("r p e t -> r p (e t)"),
                                      diag[:].rearrange("r e t -> r (e t)").unsqueeze(1).to_broadcast([2, PAIRS, 2 * N])).then_inc(ones_loaded, 16)

            walk(act, step)

        @block.tensor
        def _(pe):
            def transpose_x(u, s, first):
                pe.wait_ge(xn_done, u + 1)
                if not first:
                    pe.wait_ge(xt_lo, u)
                for k in range(DK):
                    for t in range(UT):
                        last = nc.tensor.transpose(ps_x[:, k, P * t:P * (t + 1)], xn[s][:, t, P * k:P * (k + 1)], ident[:])
                last.then_inc(xt_ready, 1)

            def project_q(u, s, first):
                pe.wait_ge(xt_lo, u + 1)
                if not first:
                    pe.wait_ge(q_lo, 2 * u)
                for e in range(2):
                    cols = slice(P * e, P * (e + 1))
                    for n, (w, v) in enumerate(((wq_h, xt_h), (wq_l, xt_h), (wq_h, xt_l))):
                        for k in range(DK):
                            last = nc.tensor.matmul(ps_q[:, e, :], w[:, k, cols], v[s][:, k, :],
                                                    start=(n + k == 0), stop=(n == 2 and k == DK - 1))
                last.then_inc(q_ready, 1)

            def project_k(u, s, first):
                if first:
                    pe.wait_ge(first_ctx_lo, 2)
                    pe.wait_ge(w_lo, 2)
                else:
                    pe.wait_ge(ctx_split, 4 * u)
                    pe.wait_ge(k_lo, 2 * u)
                for e in range(2):
                    cols = slice(P * e, P * (e + 1))
                    for n, (w, v) in enumerate(((wk_h, ctx_h), (wk_l, ctx_h), (wk_h, ctx_l))):
                        for k, rows in ((0, P), (1, C - P)):
                            last = nc.tensor.matmul(ps_k[:, e, :], w[0:rows, k, cols], v[s][0:rows, k, :],
                                                    start=(n + k == 0), stop=(n == 2 and k == DK - 1))
                last.then_inc(k_ready, 1)

            def project_v(u, s, first):
                if not first:
                    pe.wait_ge(v_copied, u)
                for t in range(UT):
                    for n, (v, w) in enumerate(((ctx_h, wv_h), (ctx_h, wv_l), (ctx_l, wv_h))):
                        for k, rows in ((0, P), (1, C - P)):
                            last = nc.tensor.matmul(ps_v[:, t // 2, D * (t % 2):D * (t % 2 + 1)],
                                                    v[s][0:rows, k, P * t:P * (t + 1)], w[0:rows, k, :],
                                                    start=(n + k == 0), stop=(n == 2 and k == DK - 1))
                last.then_inc(v_ready, 1)

            def step(u, s, turn, has):
                project_k(u, s, not has(-1))
                if not has(-1):
                    pe.wait_ge(consts_ready, 3)
                    transpose_x(0, 0, True)
                    pe.wait_ge(w_lo, 4)
                    project_v(0, 0, True)
                    pe.wait_ge(w_lo, 6)
                project_q(u, s, not has(-1))
                if has(1):
                    transpose_x(u + 1, 1 - s, False)
                if has(-1):
                    project_v(u, s, False)

            walk(pe, step)


def attend_and_feed(nc, x1, ident, bo_bc, wo_h, wo_l, q_dram, k_dram, v_all, q_stack, k_stack, v_pad,
                    wg, wu, wd, w16, w_large, out, half, eps, norm_buffers, late, w_split, ctx_odd, qk_odd,
                    q_stored, k_stored, qk_loaded):
    stack = ExitStack()
    with stack:
        def sb(name, shape, dt):
            return stack.enter_context(nc.sbuf_tensor(name, shape, dt))

        def sem(name):
            return stack.enter_context(nc.semaphore(name))

        probs = [sb(f"probs{i}", [P, 2, 2, 2, N], F32) for i in range(2)]
        neg_max = [sb(f"neg_max{i}", [P, P], F32) for i in range(2)]
        max_t = [sb(f"max_t{i}", [2 * H, P], F16) for i in range(2)]
        o_t = sb("o_t", [P, GROUPS, N], F32)
        rsum = [sb(f"rsum{i}", [P, H], F32) for i in range(2)]
        o_n = [sb(f"o_n{i}", [P, H, HD], F32) for i in range(2)]
        ot_h = sb("ot_h", [P, DK, N], F16)
        ot_l = sb("ot_l", [P, DK, N], F16)

        ps_s = [stack.enter_context(nc.psum_tensor(f"ps_s{i}", [P, 2, 2, N], F32)) for i in range(2)]
        ps_ms = stack.enter_context(nc.psum_tensor("ps_ms", [P, 2, 2, N], F32))
        ps_oc = stack.enter_context(nc.psum_tensor("ps_oc", [P, 2, 2 * N], F32))
        ps_m = [ps_ms[:, e] for e in range(2)]
        ps_o, ps_c = ps_oc[:, 0], ps_oc[:, 1]

        w_max = sb("w_max", [P, 4], F32)
        w_top = sb("w_top", [P, 1], F32)
        w_loaded = [sem(f"w_loaded{n}") for n in range(2)]
        w32_loaded, w32_made = sem("w32_loaded"), sem("w32_made")
        w_made, w_max_done, w_flag = sem("w_made"), sem("w_max_done"), sem("w_flag")
        max_loaded = [sem(f"max_loaded{i}") for i in range(RING)]
        max_cleared, v_padded, bo_added = sem("max_cleared"), sem("v_padded"), sem("bo_added")
        half_scored, half_reduced = sem("half_scored"), sem("half_reduced")
        max_transposed, max_copied = sem("max_transposed"), sem("max_copied")
        pair_scored, pair_exp = sem("pair_scored"), sem("pair_exp")
        pv_ready, pv_copied = sem("pv_ready"), sem("pv_copied")
        back_ready, recip_done, normed = sem("back_ready"), sem("recip_done"), sem("normed")
        ot_ready, ot_hi, ot_lo = sem("ot_ready"), sem("ot_hi"), sem("ot_lo")
        wo_ready, res_done = sem("wo_ready"), sem("res_done")

        LOOPS = 3

        def walk_batches(eng, start, step):
            for i in range(start):
                step(i, i, lambda d: (i + d) // RING, lambda d: i + d >= 0)
            with eng.Fori(0, LOOPS) as j:
                for k in range(start, start + RING):
                    step(RING * j + k, k, lambda d: j + (k + d) // RING, lambda d: True)
            for i in range(start + LOOPS * RING, B):
                step(i, i, lambda d: (i + d) // RING, lambda d: i + d < B)

        wq_h, wq_l, wk_h, wk_l, wv_h, wv_l = w_split
        last_ctx_h, last_ctx_l = ctx_odd
        last_q_h, last_q_l, last_k_h, last_k_l = qk_odd
        last_v_ready, last_v_copied = sem("last_v_ready"), sem("last_v_copied")
        last_k_ready, last_k_hi, last_k_lo = sem("last_k_ready"), sem("last_k_hi"), sem("last_k_lo")
        last_q_ready, last_q_hi, last_q_lo = sem("last_q_ready"), sem("last_q_hi"), sem("last_q_lo")

        stats, mean_var, rstd, var_eps, xn, xt_h, xt_l = norm_buffers
        last_xt_h, last_xt_l = xt_h[1], xt_l[1]

        def w_chunk(c):
            parts, cols = w16[c // 2].shape[1] // 2, w16[c // 2].shape[2]
            return xn[c % 2][:].rearrange("p t d -> p (t d)")[:, 0:parts * cols].bitcast(I32).rearrange("p (k n) -> p k n", k=parts)

        w32 = [k_stack[n][:].rearrange("p a e t -> p (a e t)").bitcast(F32)[:, 0:DK * FF]
               .rearrange("p (k n) -> p k n", n=w16[n].shape[2]) for n in range(3)]
        silu = [sb(f"feed_silu{i}", [P, U], F32) for i in range(2)]
        assert 2 * FT * U + 2 * DK * U <= TILES * D
        v_flat = v_all[:].rearrange("p t n -> p (t n)")
        hid_f = [v_flat[:, FT * U * i:FT * U * (i + 1)].rearrange("p (f t) -> p f t", f=FT) for i in range(2)]
        xt_f = [v_flat[:, 2 * FT * U + DK * U * i:2 * FT * U + DK * U * (i + 1)].rearrange("p (k t) -> p k t", k=DK)
                for i in range(2)]
        hid_h = [late[:, FT * U * i:FT * U * (i + 1)].rearrange("p (f t) -> p f t", f=FT) for i in range(2)]
        hid_l = [late[:, 2 * FT * U:].rearrange("p (f t) -> p f t", f=FT),
                 probs[1][:].rearrange("p a e k q -> p (a e k q)")[:, 0:FT * U // 2].bitcast(F16)
                 .rearrange("p (f t) -> p f t", f=FT)]

        ps_x = ps_ms[:].rearrange("p e h k -> p e (h k)")
        ps_g = [ps_s[i][:, 0].rearrange("p k q -> p (k q)") for i in range(2)]
        ps_u = [ps_s[i][:, 1].rearrange("p k q -> p (k q)") for i in range(2)]
        ps_y = ps_oc[:].rearrange("p a (t d) -> p (a t) d", t=2)

        stats_done, mv_done, var_done, rstd_done, xn_done = (sem("feed_" + n) for n in (
            "stats_done", "mv_done", "var_done", "rstd_done", "xn_done"))
        xt_ready, xt_full, xt_hi, xt_lo = sem("feed_xt_ready"), sem("feed_xt_full"), sem("feed_xt_hi"), sem("feed_xt_lo")
        gu_ready, silu_done, hid_done, hid_hi, hid_lo = (sem("feed_" + n) for n in (
            "gu_ready", "silu_done", "hid_done", "hid_hi", "hid_lo"))
        y_ready, y_done = sem("feed_y_ready"), sem("feed_y_done")
        stored = [sem(f"feed_stored{i}") for i in range(2)]

        def walk_units(eng, step):
            for u in range(2):
                step(u, u % 2, lambda d: u + d >= 0)
            with eng.Fori(1, NU // 2 - 1) as j:
                for s in range(2):
                    step(2 * j + s, s, lambda d: True)
            for u in range(NU - 2, NU):
                step(u, u % 2, lambda d: u + d < NU)

        block = stack.enter_context(nc.Block())

        @block.sync
        def _(sp):
            def load_max(b, r):
                sp.wait_ge(max_copied, b + 1)
                sp.dma_start(q_stack[r][ROW_MAX:ROW_MAX + 2, :, :], max_t[r % 2][:]).then_inc(max_loaded[r], 16)

            def load_w_chunk(c):
                w, parts = (wg, wu, wd)[c // 2], w16[c // 2].shape[1] // 2
                if c >= 2:
                    sp.wait_ge(w_made, c - 1)
                sp.dma_start(w_chunk(c), w.rearrange("(k p) n -> p k n", p=P)[:, parts * (c % 2):parts * (c % 2 + 1)]).then_inc(w_loaded[c % 2], 16)

            def step(i, r, turn, has):
                if not has(-1):
                    load_w_chunk(2)
                    load_w_chunk(3)
                if has(3) and has(-1):
                    sp.wait_ge(pair_scored, PAIRS * i)
                    load_qk(sp, i + 3, (r + 3) % RING, q_dram, k_dram, q_stack, k_stack, qk_loaded)
                if has(1):
                    load_max(i + 1, (r + 1) % RING)
                if not has(-1):
                    load_w_chunk(4)
                    load_w_chunk(5)

            load_qk(sp, 1, 1, q_dram, k_dram, q_stack, k_stack, qk_loaded)
            sp.wait_ge(k_stored[1], 32)
            sp.wait_ge(q_stored[1], 32)
            load_qk(sp, 2, 2, q_dram, k_dram, q_stack, k_stack, qk_loaded)
            last = bass.ds(B - 2, 2)
            sp.wait_ge(last_k_hi, 2)
            sp.dma_start(k_dram[last, :, 0].rearrange("b e p t -> p (b e) t"),
                         last_k_h.rearrange("p b e t -> p (b e) t")).then_inc(k_stored[1], 16)
            sp.wait_ge(last_k_lo, 2)
            sp.dma_start(k_dram[last, :, 1].rearrange("b e p t -> p (b e) t"),
                         last_k_l.rearrange("p b e t -> p (b e) t")).then_inc(k_stored[1], 16)
            load_max(0, 0)
            sp.wait_ge(last_q_hi, 2)
            sp.dma_start(q_dram[last, :, 0].rearrange("b e p t -> p (b e) t"),
                         last_q_h.rearrange("p b e t -> p (b e) t")).then_inc(q_stored[1], 16)
            sp.wait_ge(last_q_lo, 2)
            sp.dma_start(q_dram[last, :, 1].rearrange("b e p t -> p (b e) t"),
                         last_q_l.rearrange("p b e t -> p (b e) t")).then_inc(q_stored[1], 16)
            load_qk(sp, 3, 3, q_dram, k_dram, q_stack, k_stack, qk_loaded)
            load_w_chunk(0)
            load_w_chunk(1)
            for s in range(2):
                sp.wait_ge(q_stored[s], 32 * NU // 2)
                sp.wait_ge(k_stored[s], 32 * NU // 2)
            walk_batches(sp, 1, step)
            for r in range(RING):
                sp.wait_ge(qk_loaded[r], 16 * QK_DMAS * B // RING)
                sp.wait_ge(max_loaded[r], 16 * B // RING)

            sp.wait_ge(pair_scored, PAIRS * B)
            for n, w in enumerate((wg, wu, wd)):
                sp.dma_start(w32[n].bitcast(I32), w.rearrange("(k p) n -> p k n", p=P)).then_inc(w32_loaded, 16)

            def unit_step(u, s, has):
                sp.wait_ge(y_done, u + 1)
                sp.dma_start(out[bass.ds(U * u, U), :].rearrange("(t p) d -> p t d", p=P),
                             x1[:, bass.ds(UT * u, UT), :]).then_inc(stored[s], 16)

            walk_units(sp, unit_step)
            for s in range(2):
                sp.wait_ge(stored[s], 16 * NU // 2)

        @block.gpsimd
        def _(pool):
            def pad_v(b, r):
                nc.gpsimd.tensor_copy(v_pad[r][:, :, :, 0:HD],
                                      v_all[:, bass.ds(2 * b, 2), :].rearrange("p t (h d) -> p t h d", h=H)).then_inc(v_padded, 1)

            def add_bo(b):
                for t in range(2):
                    tile = x1[:, bass.ds(2 * b + t, 1), :].rearrange("p a d -> p (a d)")
                    nc.gpsimd.tensor_tensor(tile, tile, bo_bc[:], ALU.add).then_inc(bo_added, 1)

            def step(i, r, turn, has):
                if has(3) and has(-1):
                    pool.wait_ge(pv_ready, GROUPS * i)
                if has(2):
                    add_bo(i + 2)
                if has(3):
                    pad_v(i + 3, (r + 3) % RING)

            for n in range(2):
                nc.gpsimd.memset(neg_max[n][:], 0.0).then_inc(max_cleared, 1)
            for b in range(3):
                pad_v(b, b)
            for b in range(2):
                add_bo(b)
            pool.wait_ge(last_v_copied, 2)
            for c in range(6):
                parts = w16[c // 2].shape[1] // 2
                pool.wait_ge(w_loaded[c % 2], 16 * (c // 2 + 1))
                nc.gpsimd.tensor_copy(w16[c // 2][:, parts * (c % 2):parts * (c % 2 + 1), :], w_chunk(c)).then_inc(w_made, 1)
            walk_batches(pool, 1, step)
            pool.wait_ge(w_max_done, 4)
            nc.gpsimd.partition_all_reduce(w_top[:], w_max[:, 3:4], P, bass.bass_isa.ReduceOp.max).then_inc(w_flag, 1)
            pool.wait_ge(w_flag, 1)
            nc.gpsimd.tensor_scalar(w_large[:], w_top[:], INT_EXACT, None, ALU.is_ge).then_inc(w_flag, 1)
            pool.wait_ge(w_flag, 2)

            def rstd_unit(u, s):
                pool.wait_ge(mv_done, u + 1)
                nc.gpsimd.tensor_tensor(var_eps[:], mean_var[s][:, :, 1], eps[:], ALU.add).then_inc(var_done, 1)
                pool.wait_ge(var_done, u + 1)
                nc.gpsimd.tensor_tensor(rstd[s][:], var_eps[:], half[:], ALU.pow).then_inc(rstd_done, 1)
                pool.wait_ge(rstd_done, u + 1)

            def unit_step(u, s, has):
                if has(2):
                    rstd_unit(u + 2, s)

            rstd_unit(0, 0)
            rstd_unit(1, 1)
            pool.wait_ge(w32_loaded, 48)
            for n in range(3):
                nc.gpsimd.tensor_copy(w32[n], w32[n].bitcast(I32)).then_inc(w32_made, 1)
            walk_units(pool, unit_step)

        @block.vector
        def _(dve):
            def reduce_pair(b, r, p, first):
                cols = neg_max[r % 2][:, 0:2 * H].rearrange("q (e p h) -> q p h e", e=2, p=PAIRS)
                for h in range(2):
                    dve.wait_ge(half_scored, H * b + 2 * p + h + 1)
                    if p == 0 and h == 0 and not first:
                        dve.wait_ge(max_transposed, b - 1)
                    nc.vector.tensor_reduce(cols[:, p, h], ps_m[h], AXX, ALU.max,
                                            negate=True).then_inc(half_reduced, 1)

            def normalise(b, h):
                dve.wait_ge(back_ready, 2 * b + h + 1)
                dve.wait_ge(normed, 2 * b)
                heads = ps_c.rearrange("p (h c) -> p h c", h=H)
                nc.vector.reciprocal(rsum[h][:], heads[:, :, HD]).then_inc(recip_done, 1)
                dve.wait_ge(recip_done, 2 * b + h + 1)
                dve.wait_ge(ot_ready, b)
                nc.vector.tensor_tensor(o_n[h][:], heads[:, :, 0:HD],
                                        rsum[h][:].unsqueeze(2).to_broadcast([P, H, HD]), ALU.mult).then_inc(normed, 1)

            def ot_low(b):
                dve.wait_ge(ot_hi, b + 1)
                nc.vector.tensor_tensor(ot_l[:].rearrange("p k t -> p (k t)"), ps_c,
                                        ot_h[:].rearrange("p k t -> p (k t)"), ALU.subtract).then_inc(ot_lo, 1)

            def residual_attn(b):
                dve.wait_ge(wo_ready, b + 1)
                dve.wait_ge(bo_added, 2 * b + 2)
                tiles = x1[:, bass.ds(2 * b, 2), :].rearrange("p t d -> p (t d)")
                nc.vector.scalar_tensor_tensor(out=tiles, in0=ps_c, scalar=1.0 / WS, in1=tiles,
                                               op0=ALU.mult, op1=ALU.add).then_inc(res_done, 1)

            def step(i, r, turn, has):
                for p in range(PAIRS):
                    if 4 <= p < 7 and has(1) and not has(2):
                        dve.wait_ge(w_made, 2 * (p - 4) + 2)
                        w = w16[p - 4][:]
                        nc.vector.tensor_reduce(w_max[:, p - 4:p - 3], w.rearrange("p k n -> p (k n)"), AXX, ALU.max,
                                                apply_absolute_value=True).then_inc(w_max_done, 1)
                    if p == 7 and has(1) and not has(2):
                        dve.wait_ge(w_max_done, 3)
                        nc.vector.tensor_reduce(w_max[:, 3:4], w_max[:, 0:3], AXX, ALU.max).then_inc(w_max_done, 1)
                    if p < 4 and has(1):
                        reduce_pair(i + 1, (r + 1) % RING, p + 4, False)
                    if p >= 4 and has(2):
                        reduce_pair(i + 2, (r + 2) % RING, p - 4, False)
                    if has(-1):
                        if p in (1, 2):
                            normalise(i - 1, p - 1)
                        if p == 4:
                            ot_low(i - 1)
                        if p == 7:
                            residual_attn(i - 1)
                    if not has(1):
                        if p == 0:
                            stats_unit(0, 0, True)
                        if p == 1:
                            dve.wait_ge(stats_done, 1)
                            aggregate_unit(0, 0)
                        if p == 3:
                            normalise_unit(0, 0, True)
                        if p == 5:
                            stats_unit(1, 1, True)
                        if p == 6:
                            dve.wait_ge(stats_done, 2)
                            aggregate_unit(1, 1)
                        if p == 7:
                            xt_low(0, 0)

            def stats_unit(u, s, first):
                if not first:
                    dve.wait_ge(mv_done, u - 1)
                    dve.wait_ge(xn_done, u - 1)
                    dve.wait_ge(rstd_done, u - 1)
                for t in range(UT):
                    last = nc.vector.bn_stats(stats[s][:, t, :], x1[:, bass.ds(UT * u + t, 1), :].rearrange("p a d -> p (a d)"))
                last.then_inc(stats_done, 1)

            def aggregate_unit(u, s):
                for t in range(UT):
                    last = nc.vector.bn_aggr(mean_var[s][:, t, :], stats[s][:, t, :])
                last.then_inc(mv_done, 1)

            def normalise_unit(u, s, first):
                dve.wait_ge(rstd_done, u + 1)
                if not first:
                    dve.wait_ge(xt_ready, u - 1)
                for t in range(UT):
                    last = nc.vector.tensor_scalar(xn[s][:, t, :], x1[:, bass.ds(UT * u + t, 1), :].rearrange("p a d -> p (a d)"),
                                                   mean_var[s][:, t, 0:1], rstd[s][:, t:t + 1],
                                                   ALU.subtract, ALU.mult)
                last.then_inc(xn_done, 1)

            def xt_low(u, s):
                dve.wait_ge(xt_hi, u + 1)
                nc.vector.tensor_tensor(xt_l[s][:], ps_x, xt_h[s][:], ALU.subtract).then_inc(xt_lo, 1)

            def hidden(u, s, f, first):
                dve.wait_ge(silu_done, FT * u + f + 1)
                if f == 0 and first:
                    dve.wait_ge(v_padded, B)
                if f == 0 and not first:
                    dve.wait_ge(y_ready, u - 1)
                    dve.wait_ge(hid_hi, FT * (u - 1))
                nc.vector.scalar_tensor_tensor(out=hid_f[s][:, f, :], in0=ps_u[f % 2], scalar=W_SCALE * HS,
                                               in1=silu[f % 2][:], op0=ALU.mult, op1=ALU.mult).then_inc(hid_done, 1)

            def hidden_low(u, s, f):
                dve.wait_ge(hid_hi, FT * u + f + 1)
                nc.vector.tensor_tensor(hid_l[s][:, f, :], hid_f[s][:, f, :], hid_h[s][:, f, :],
                                        ALU.subtract).then_inc(hid_lo, 1)

            def residual_ff(u):
                dve.wait_ge(y_ready, u + 1)
                tiles = x1[:, bass.ds(UT * u, UT), :].rearrange("p t d -> p (t d)")
                nc.vector.scalar_tensor_tensor(out=tiles, in0=ps_y.rearrange("p t d -> p (t d)"),
                                               scalar=W_SCALE / HS, in1=tiles,
                                               op0=ALU.mult, op1=ALU.add).then_inc(y_done, 1)

            def unit_step(u, s, has):
                for f in range(FT):
                    hidden(u, s, f, not has(-2))
                    if not has(-1):
                        if f in (1, 2):
                            normalise(B - 1, f - 1)
                        if f == 4:
                            ot_low(B - 1)
                        if f == 5:
                            residual_attn(B - 1)
                    if f == 0 and has(1):
                        normalise_unit(u + 1, 1 - s, not has(-1))
                    if f > 0:
                        hidden_low(u, s, f - 1)
                    if f == 3:
                        if has(1):
                            xt_low(u + 1, 1 - s)
                        if has(2):
                            stats_unit(u + 2, s, False)
                            dve.wait_ge(stats_done, u + 3)
                        if has(-1):
                            residual_ff(u - 1)
                        if has(2):
                            aggregate_unit(u + 2, s)
                hidden_low(u, s, FT - 1)

            def last_low(e, ps, hi, lo, scale, high, low):
                dve.wait_ge(high, e + 1)
                nc.vector.scalar_tensor_tensor(out=lo[:, :, e], in0=ps[:, e], scalar=scale,
                                               in1=hi[:, :, e], op0=ALU.mult, op1=ALU.subtract).then_inc(low, 1)

            dve.wait_ge(max_cleared, 2)
            for n in range(PAIRS + 4):
                reduce_pair(n // PAIRS, n // PAIRS, n % PAIRS, True)
                if n in (1, 3):
                    last_low((n - 1) // 2, ps_s[0], last_k_h, last_k_l, 1.0 / WS, last_k_hi, last_k_lo)
                if n in (5, 7):
                    last_low((n - 5) // 2, ps_s[1], last_q_h, last_q_l, SC / WS, last_q_hi, last_q_lo)
            walk_batches(dve, 2, step)

            walk_units(dve, unit_step)
            residual_ff(NU - 1)

        @block.scalar
        def _(act):
            def exp_pair(b, p, first):
                g = p // 2
                act.wait_ge(pair_scored, PAIRS * b + p + 1)
                if p % 2 == 0 and not (first and g < 2):
                    act.wait_ge(pv_ready, GROUPS * b + g - 1)
                nc.scalar.activation(probs[g % 2][:, p % 2].rearrange("p e k q -> p (e k q)"),
                                     ps_s[p % 2][:].rearrange("p e k q -> p (e k q)"), ACT.Exp).then_inc(pair_exp, 1)

            def copy_pv(b, g, first):
                act.wait_ge(pv_ready, GROUPS * b + g + 1)
                if g == 0 and not first:
                    act.wait_ge(back_ready, 2 * b)
                nc.scalar.activation(o_t[:, g, :], ps_o[:, 0:N], ACT.Copy).then_inc(pv_copied, 1)

            def ot_high(b, first):
                act.wait_ge(ot_ready, b + 1)
                if not first:
                    act.wait_ge(wo_ready, b)
                nc.scalar.activation(ot_h[:].rearrange("p k t -> p (k t)"), ps_c, ACT.Copy).then_inc(ot_hi, 1)

            def copy_max(b, r, turn):
                act.wait_ge(max_transposed, b + 1)
                if turn is not None:
                    act.wait_ge(max_loaded[(r + 2) % RING], 16 * turn)
                nc.scalar.activation(max_t[r % 2][:], ps_o[0:2 * H, N:N + P], ACT.Copy).then_inc(max_copied, 1)

            def step(i, r, turn, has):
                for p in range(PAIRS):
                    if p == 0 and has(-1):
                        copy_pv(i - 1, 3, False)
                    if has(0):
                        if p in (2, 4, 6):
                            copy_pv(i, p // 2 - 1, not has(-1))
                        exp_pair(i, p, not has(-1))
                    if p == 3 and has(-1):
                        ot_high(i - 1, not has(-2))
                    if p == 4 and has(1):
                        copy_max(i + 1, (r + 1) % RING, turn(-1) + 1 if has(-1) else None)
                    if p == 5 and not has(1):
                        xt_copy(0, 0, True)

            def xt_copy(u, s, first):
                act.wait_ge(xt_ready, u + 1)
                if first:
                    act.wait_ge(v_padded, B)
                else:
                    act.wait_ge(gu_ready, FT * (u - 1))
                nc.scalar.activation(xt_f[s][:], ps_x, ACT.Copy).then_inc(xt_full, 1)
                nc.scalar.activation(xt_h[s][:], ps_x, ACT.Copy).then_inc(xt_hi, 1)

            def gate_silu(u, f, first):
                act.wait_ge(gu_ready, FT * u + f + 1)
                if not (first and f < 2):
                    act.wait_ge(hid_done, FT * u + f - 1)
                nc.scalar.activation(silu[f % 2][:], ps_g[f % 2], ACT.Silu, scale=W_SCALE).then_inc(silu_done, 1)

            def hidden_high(u, s, f, first):
                act.wait_ge(hid_done, FT * u + f + 1)
                if f == 0 and not first:
                    act.wait_ge(y_ready, u - 1)
                    act.wait_ge(hid_lo, FT * (u - 1))
                nc.scalar.activation(hid_h[s][:, f, :], hid_f[s][:, f, :], ACT.Copy).then_inc(hid_hi, 1)

            def unit_step(u, s, has):
                for f in range(FT):
                    gate_silu(u, f, not has(-1))
                    if f == 0 and not has(-1):
                        copy_pv(B - 1, GROUPS - 1, False)
                    if f == 4 and not has(-1):
                        ot_high(B - 1, False)
                    if f > 0:
                        hidden_high(u, s, f - 1, not has(-2))
                    if f == 2 and has(1):
                        xt_copy(u + 1, 1 - s, not has(-1))
                hidden_high(u, s, FT - 1, False)

            def last_high(e, ps, hi, scale, ready, high):
                act.wait_ge(ready, e + 1)
                nc.scalar.activation(hi[:, :, e], ps[:, e], ACT.Copy, scale=scale).then_inc(high, 1)

            act.wait_ge(k_stored[1], 32 * (NU // 2 - 1))
            act.wait_ge(q_stored[1], 32 * (NU // 2 - 1))
            last_high(0, ps_s[0], last_k_h, 1.0 / WS, last_k_ready, last_k_hi)
            last_high(1, ps_s[0], last_k_h, 1.0 / WS, last_k_ready, last_k_hi)
            last_high(0, ps_s[1], last_q_h, SC / WS, last_q_ready, last_q_hi)
            last_high(1, ps_s[1], last_q_h, SC / WS, last_q_ready, last_q_hi)
            copy_max(0, 0, None)
            for h in range(2):
                act.wait_ge(last_v_ready, 2 * h + 2)
                nc.scalar.activation(v_all[:, TILES - 4 + 2 * h:TILES - 2 + 2 * h, :].rearrange("p t n -> p (t n)"),
                                     ps_s[0][:, h].rearrange("p a b -> p (a b)"), ACT.Copy, scale=1.0 / WS).then_inc(last_v_copied, 1)
            walk_batches(act, 2, step)

            walk_units(act, unit_step)

        @block.tensor
        def _(pe):
            def score_for_max(b, r, turn, p, first, halves=(0, 1)):
                if p == 0 and 0 in halves:
                    pe.wait_ge(qk_loaded[r], 16 * QK_DMAS * (turn + 1))
                for h in halves:
                    if not (first and p == 0):
                        pe.wait_ge(half_reduced, H * b + 2 * p + h - 1)
                    nc.tensor.matmul(ps_m[h].rearrange("q e k -> q (e k)"), q_stack[r][0:ROW_MAX, p, P * h:P * (h + 1)],
                                     k_stack[r][0:ROW_MAX, p, :, :].rearrange("r e k -> r (e k)"),
                                     start=True, stop=True).then_inc(half_scored, 1)

            def score_pair(b, r, turn, p, first):
                if p == 0:
                    pe.wait_ge(max_loaded[r], 16 * (turn + 1))
                if not (first and p < 2):
                    pe.wait_ge(pair_exp, PAIRS * b + p - 1)
                for e in range(2):
                    for k in range(2):
                        last = nc.tensor.matmul(ps_s[p % 2][:, e, k, :], k_stack[r][:, p, e, P * k:P * (k + 1)],
                                                q_stack[r][:, p, :], start=True, stop=True)
                last.then_inc(pair_scored, 1)

            def weigh_values(b, r, g, first):
                if g == 0:
                    pe.wait_ge(v_padded, b + 1)
                pe.wait_ge(pair_exp, PAIRS * b + 2 * g + 2)
                if not (first and g == 0):
                    pe.wait_ge(pv_copied, GROUPS * b + g)
                for k in range(2):
                    for h in range(4):
                        last = nc.tensor.matmul(ps_o[32 * h:32 * h + 32, 0:N], v_pad[r][:, k, 4 * g + h, :],
                                                probs[g % 2][:, h // 2, h % 2, k, :], start=(k == 0), stop=(k == 1))
                last.then_inc(pv_ready, 1)

            def transpose_max(b, r):
                pe.wait_ge(half_reduced, H * b + H)
                if not (isinstance(b, int) and b == 0):
                    pe.wait_ge(max_copied, b)
                nc.tensor.transpose(ps_o[:, N:N + P], neg_max[r % 2][:], ident[:]).then_inc(max_transposed, 1)

            def back(b, h):
                if h == 0:
                    pe.wait_ge(pv_copied, GROUPS * b + GROUPS)
                else:
                    pe.wait_ge(normed, 2 * b + 1)
                for g in range(GROUPS):
                    last = nc.tensor.transpose(ps_c[:, P * g:P * (g + 1)], o_t[:, g, P * h:P * (h + 1)], ident[:])
                last.then_inc(back_ready, 1)

            def transpose_o(b):
                pe.wait_ge(normed, 2 * b + 2)
                for k in range(DK):
                    for h in range(2):
                        last = nc.tensor.transpose(ps_c[:, N * k + P * h:N * k + P * (h + 1)],
                                                   o_n[h][:, PAIRS * k:PAIRS * (k + 1), :].rearrange("p h d -> p (h d)"), ident[:])
                last.then_inc(ot_ready, 1)

            def project_o(b, halves=(0, 1)):
                if 0 in halves:
                    pe.wait_ge(ot_lo, b + 1)
                for h in halves:
                    for n, (o, w) in enumerate(((ot_h, wo_h), (ot_h, wo_l), (ot_l, wo_h))):
                        for k in range(DK):
                            last = nc.tensor.matmul(ps_c[:, D * h:D * (h + 1)], o[:, k, P * h:P * (h + 1)], w[:, k, :],
                                                    start=(n + k == 0), stop=(n == 2 and k == DK - 1))
                if 1 in halves:
                    last.then_inc(wo_ready, 1)

            def maxima(i, r, turn, has, p, h):
                if p < 4 and has(1):
                    score_for_max(i + 1, (r + 1) % RING, turn(1), p + 4, False, (h,))
                if p >= 4 and has(2):
                    score_for_max(i + 2, (r + 2) % RING, turn(2), p - 4, False, (h,))

            def step(i, r, turn, has):
                for p in range(PAIRS):
                    maxima(i, r, turn, has, p, 0)
                    score_pair(i, r % RING, turn(0), p, not has(-1))
                    maxima(i, r, turn, has, p, 1)
                    if p == 0 and has(-1):
                        weigh_values(i - 1, (r - 1) % RING, 3, False)
                    if p in (1, 2) and has(-1):
                        if p == 1:
                            pe.wait_ge(res_done, i - 1)
                        back(i - 1, p - 1)
                    if p == 3 and has(-1):
                        transpose_o(i - 1)
                    if p == 4 and has(1):
                        transpose_max(i + 1, (r + 1) % RING)
                    if p in (5, 7) and has(-1):
                        project_o(i - 1, (p // 2 - 2,))
                    if p in (2, 4, 6) and has(0):
                        weigh_values(i, r % RING, p // 2 - 1, not has(-1))
                    if p == 4 and not has(1):
                        pe.wait_ge(half_reduced, H * B)
                        transpose_x(0, 0, True)

            def transpose_x(u, s, first):
                pe.wait_ge(xn_done, u + 1)
                if not first:
                    pe.wait_ge(xt_lo, u)
                for k in range(DK):
                    for t in range(UT):
                        last = nc.tensor.transpose(ps_x[:, k, P * t:P * (t + 1)], xn[s][:, t, P * k:P * (k + 1)], ident[:])
                last.then_inc(xt_ready, 1)

            def gate_up(u, s, f, first, split):
                if f == 0:
                    pe.wait_ge(xt_lo, u + 1)
                if first and f < 2:
                    pe.wait_ge(pair_exp, PAIRS * B - 1 + f)
                else:
                    pe.wait_ge(hid_done, FT * u + f - 1)
                for n, ps in ((0, ps_g), (1, ps_u)):
                    terms = [(w16[n], xt_h[s]), (w16[n], xt_l[s])] if split else [(w32[n], xt_f[s])]
                    for m, (w, v) in enumerate(terms):
                        for k in range(DK):
                            last = nc.tensor.matmul(ps[f % 2], w[:, k, P * f:P * (f + 1)], v[:, k, :],
                                                    start=(m + k == 0), stop=(m == len(terms) - 1 and k == DK - 1))
                last.then_inc(gu_ready, 1)

            def down(u, s, first, split):
                pe.wait_ge(hid_lo, FT * u + FT)
                if first:
                    pe.wait_ge(res_done, B)
                else:
                    pe.wait_ge(y_done, u)
                terms = [(hid_h[s], w16[2]), (hid_l[s], w16[2])] if split else [(hid_f[s], w32[2])]
                for t in range(UT):
                    for m, (v, w) in enumerate(terms):
                        for f in range(FT):
                            last = nc.tensor.matmul(ps_y[:, t, :], v[:, f, P * t:P * (t + 1)], w[:, f, :],
                                                    start=(m + f == 0), stop=(m == len(terms) - 1 and f == FT - 1))
                last.then_inc(y_ready, 1)

            def whole(split):
                def unit_step(u, s, has):
                    for f in range(FT):
                        gate_up(u, s, f, not has(-1), split)
                        if f == 2 and has(1):
                            transpose_x(u + 1, 1 - s, False)
                        if f == 3 and has(-1):
                            down(u - 1, 1 - s, not has(-2), split)
                        if not has(-1):
                            if f == 0:
                                weigh_values(B - 1, (B - 1) % RING, GROUPS - 1, False)
                            if f == 1:
                                pe.wait_ge(res_done, B - 1)
                                back(B - 1, 0)
                            if f == 2:
                                back(B - 1, 1)
                            if f == 3:
                                transpose_o(B - 1)
                            if f == 5:
                                project_o(B - 1)

                walk_units(pe, unit_step)
                down(NU - 1, 1, False, split)

            def last_v(t):
                for n, (v, w) in enumerate(((last_ctx_h, wv_h), (last_ctx_h, wv_l), (last_ctx_l, wv_h))):
                    for k, rows in ((0, P), (1, C - P)):
                        last = nc.tensor.matmul(ps_s[0][:, t // 2, t % 2, :],
                                                v[0:rows, k, P * t:P * (t + 1)], w[0:rows, k, :],
                                                start=(n + k == 0), stop=(n == 2 and k == DK - 1))
                last.then_inc(last_v_ready, 1)

            def last_k(part):
                e, second = part // 2, part % 2
                products = [(w, v, k, rows) for w, v in ((wk_h, last_ctx_h), (wk_l, last_ctx_h), (wk_h, last_ctx_l))
                            for k, rows in ((0, P), (1, C - P))]
                for n in range(3 * second, 3 * second + 3):
                    w, v, k, rows = products[n]
                    last = nc.tensor.matmul(ps_s[0][:, e].rearrange("p b t -> p (b t)"),
                                            w[0:rows, k, P * e:P * (e + 1)], v[0:rows, k, :], start=(n == 0), stop=(n == 5))
                if second:
                    last.then_inc(last_k_ready, 1)

            def last_q(part):
                e, second = part // 2, part % 2
                products = [(w, v, k) for w, v in ((wq_h, last_xt_h), (wq_l, last_xt_h), (wq_h, last_xt_l))
                            for k in range(DK)]
                for n in range(3 * second, 3 * second + 3):
                    w, v, k = products[n]
                    last = nc.tensor.matmul(ps_s[1][:, e].rearrange("p b t -> p (b t)"),
                                            w[:, k, P * e:P * (e + 1)], v[:, k, :], start=(n == 0), stop=(n == 5))
                if second:
                    last.then_inc(last_q_ready, 1)

            for n in range(PAIRS + 4):
                if n == PAIRS:
                    pe.wait_ge(last_k_lo, 2)
                (last_k, last_q, last_v)[n // 4](n % 4)
                if n == PAIRS + 1:
                    transpose_max(0, 0)
                score_for_max(n // PAIRS, n // PAIRS, 0, n % PAIRS, n < PAIRS)
            pe.wait_ge(last_q_lo, 2)
            pe.wait_ge(last_v_copied, 2)
            walk_batches(pe, 2, step)

            large = pe.value_load(w_large[0:1, 0:1], min_val=0, max_val=1)
            with pe.If(large == 0):
                whole(True)
            with pe.Else():
                pe.wait_ge(w32_made, 3)
                whole(False)


def kernel(**inputs):
    import numpy as _np
    import concourse.bacc as _bacc
    from concourse import mybir as _mybir
    from concourse.bass_utils import run_bass_kernel_spmd as _run

    def by_row(w):
        return _np.asarray(w).reshape(-1, PAIRS, 2, HD).transpose(0, 2, 3, 1).reshape(-1, H * HD)

    arrays = {
        "x": _np.asarray(inputs["x"]).reshape(B * N, D),
        "ctx_t": _np.asarray(inputs["ctx_768"]).transpose(0, 2, 1),
        "wq": by_row(inputs["L0_xattn_Wq"]),
        "wk": by_row(inputs["L0_xattn_Wk"]),
        "wv": inputs["L0_xattn_Wv"],
        "wo": inputs["L0_xattn_Wo"],
        "bo": inputs["L0_xattn_bo"],
        "wg": _np.asarray(inputs["L0_ffn_w_gate"]).T,
        "wu": _np.asarray(inputs["L0_ffn_w_up"]).T,
        "wd": _np.asarray(inputs["L0_ffn_w_down"]).T,
    }
    arrays = {f"in_{k}": _np.ascontiguousarray(v) for k, v in arrays.items()}
    nc = _bacc.Bacc("TRN2", target_bir_lowering=False, num_devices=1)
    args = [nc.dram_tensor(k, a.shape, _mybir.dt.from_np(a.dtype), kind="ExternalInput").ap()
            for k, a in arrays.items()]
    out = nc.dram_tensor("out_0_dram", (B * N, D), _mybir.dt.float32, kind="ExternalOutput").ap()
    block_program(nc, *args, out)
    r = _run(nc, [arrays], core_ids=[0])
    return r.results[0]["out_0_dram"].reshape(B, N, D)
```

```python
import concourse.bass as bass
from concourse import mybir
from contextlib import ExitStack

F32 = mybir.dt.float32
F16 = mybir.dt.float16
I32 = mybir.dt.int32
ALU = mybir.AluOpType
ACT = mybir.ActivationFunctionType
AXX = mybir.AxisListType.X

B, N, D = 16, 256, 256
C = 192
H, HD = 16, 16
FF = 768
P = 128
PAIRS = H // 2
GROUPS = H // 4
U = 512
NU = B * N // U
UT = U // P
TILES = B * N // P
DK = D // P
REST = C - P
CTX_TERMS = 5
assert 2 * REST == P
FT = FF // P
EPS = 1e-5
WS = 16.0
SC = float(HD) ** -0.5
HS = 1.0 / 16.0
W_SCALE = 1.0 / 127.0
INT_EXACT = 2048.0
ROW_MAX = 126
RING = 4
QK_DMAS = 8


def early(u):
    return isinstance(u, int) and u < 2


def block_program(nc, x, ctx_t, wq, wk, wv, wo, bo, wg, wu, wd, out):
    stack = ExitStack()
    with stack:
        def sb(name, shape, dt):
            return stack.enter_context(nc.sbuf_tensor(name, shape, dt))

        def sem(name):
            return stack.enter_context(nc.semaphore(name))

        x1 = sb("x1", [P, TILES, D], F32)
        ident = sb("ident", [P, P], F32)
        half = sb("half", [P, UT], F32)
        eps = sb("eps", [P, UT], F32)
        bo_bc = sb("bo_bc", [P, D], F32)
        wo_h = sb("wo_h", [P, DK, D], F16)
        wo_l = sb("wo_l", [P, DK, D], F16)
        q_dram = nc.dram_tensor("q_split", (B, 2, 2, P, N), F16, kind="Internal").ap()
        k_dram = nc.dram_tensor("k_split", (B, 2, 2, P, N), F16, kind="Internal").ap()

        shapes = ([P, DK, FF], [P, DK, FF], [P, FT, D])
        w16 = [sb(f"w16_{n}", shape, F16) for n, shape in enumerate(shapes)]
        w_large = sb("w_large", [P, 1], I32)
        v_all = sb("v_all", [P, TILES, D], F32)
        q_stack = [sb(f"q_stack{i}", [P, PAIRS, N], F16) for i in range(RING)]
        k_stack = [sb(f"k_stack{i}", [P, PAIRS, 2, N], F16) for i in range(RING)]
        v_pad = [sb(f"v_pad{i}", [P, 2, H, 32], F32) for i in range(RING)]

        stats = [sb(f"stats{i}", [P, UT, 6], F32) for i in range(2)]
        mean_var = [sb(f"mean_var{i}", [P, UT, 2], F32) for i in range(2)]
        rstd = [sb(f"rstd{i}", [P, UT], F32) for i in range(2)]
        var_eps = sb("var_eps", [P, UT], F32)
        xn = [sb(f"xn{i}", [P, UT, D], F32) for i in range(2)]
        xt_h = [sb(f"xt_h{i}", [P, DK, U], F16) for i in range(2)]
        xt_l = [sb(f"xt_l{i}", [P, DK, U], F16) for i in range(2)]
        norm_buffers = (stats, mean_var, rstd, var_eps, xn, xt_h, xt_l)
        late = sb("late", [P, 3 * FT * U], F16)
        w_split = [late[:, DK * D * i:DK * D * (i + 1)].rearrange("p (k n) -> p k n", k=DK) for i in range(6)]
        rest = late[:, 6 * DK * D:]
        ctx_odd = [rest[:, DK * U * i:DK * U * (i + 1)].rearrange("p (k t) -> p k t", k=DK) for i in range(2)]
        qk_odd = [rest[:, DK * U * (i + 2):DK * U * (i + 3)].rearrange("p (b e t) -> p b e t", b=2, e=2)
                  for i in range(4)]
        q_stored = [sem(f"q_stored{i}") for i in range(2)]
        k_stored = [sem(f"k_stored{i}") for i in range(2)]
        qk_loaded = [sem(f"qk_loaded{i}") for i in range(RING)]

        project(nc, x, ctx_t, wq, wk, wv, wo, bo, x1, ident, half, eps, bo_bc, wo_h, wo_l, q_dram, k_dram,
                v_all, q_stack, k_stack, v_pad, norm_buffers, w_split, ctx_odd, qk_odd, q_stored, k_stored,
                qk_loaded)
        attend_and_feed(nc, x1, ident, bo_bc, wo_h, wo_l, q_dram, k_dram, v_all, q_stack, k_stack, v_pad,
                        wg, wu, wd, w16, w_large, out, half, eps, norm_buffers, late, w_split, ctx_odd,
                        qk_odd, q_stored, k_stored, qk_loaded)


def ctx_terms(w_h, w_l, c_h, c_l):
    return [(w_h, c_h, 0, P), (w_l, c_h, 0, P), (w_h, c_l, 0, P), (w_h, c_h, 1, P), (w_h, c_l, 1, REST)]


def load_qk(sp, b, r, q_dram, k_dram, q_stack, k_stack, qk_loaded):
    for e in range(2):
        def rows(a, first, n):
            return a[64 * e + first:64 * e + first + n]
        q_place, k_place = q_stack[r][:], k_stack[r][:, :, e, :]
        q_src = q_dram[bass.ds(b, 1), e].rearrange("b l (r p) t -> (b l r) p t", p=PAIRS)
        k_src = k_dram[bass.ds(b, 1), e].rearrange("b l (r p) t -> (b l r) p t", p=PAIRS)
        sp.dma_start(rows(q_place, 0, 2 * HD), q_src).then_inc(qk_loaded[r], 16)
        sp.dma_start(rows(q_place, 2 * HD, HD), q_src[0:HD]).then_inc(qk_loaded[r], 16)
        sp.dma_start(rows(k_place, HD, 2 * HD), k_src).then_inc(qk_loaded[r], 16)
        sp.dma_start(rows(k_place, 0, HD), k_src[0:HD]).then_inc(qk_loaded[r], 16)


def project(nc, x, ctx_t, wq, wk, wv, wo, bo, x1, ident, half, eps, bo_bc, wo_h, wo_l, q_dram, k_dram,
            v_all, q_stack, k_stack, v_pad, norm_buffers, w_split, ctx_odd, qk_odd, q_stored, k_stored, qk_loaded):
    stack = ExitStack()
    with stack:
        def sb(name, shape, dt):
            return stack.enter_context(nc.sbuf_tensor(name, shape, dt))

        def sem(name):
            return stack.enter_context(nc.semaphore(name))

        w_raw = [sb(f"w_raw{i}", [P, DK, D], F32) for i in range(4)]
        wq_h, wq_l, wk_h, wk_l, wv_h, wv_l = w_split
        ctx_raw = [sb(f"ctx_raw{i}", [P, DK, U], F32) for i in range(2)]
        ctx_h = [sb("ctx_h0", [P, DK, U], F16)[:], ctx_odd[0]]
        ctx_l = [sb("ctx_l0", [P, DK, U], F16)[:], ctx_odd[1]]
        stats, mean_var, rstd, var_eps, xn, xt_h, xt_l = norm_buffers
        q_h, q_l, k_h, k_l = ([sb(f"{n}0", [P, 2, 2, N], F16)[:], odd]
                              for n, odd in zip(("q_h", "q_l", "k_h", "k_l"), qk_odd))

        ps_x = stack.enter_context(nc.psum_tensor("ps_x", [P, DK, U], F32))
        ps_q = stack.enter_context(nc.psum_tensor("ps_q", [P, 2, U], F32))
        ps_k = stack.enter_context(nc.psum_tensor("ps_k", [P, 2, U], F32))
        ps_v = stack.enter_context(nc.psum_tensor("ps_v", [P, 2, U], F32))

        w_loaded = [sem(f"w_loaded_{n}") for n in ("k", "v", "q", "o")]
        first_loaded, bo_loaded = sem("first_loaded"), sem("bo_loaded")
        x_loaded = [sem(f"x_loaded{i}") for i in range(2)]
        ctx_loaded = [sem(f"ctx_loaded{i}") for i in range(2)]
        q_zeroed = sem("q_zeroed")
        consts_ready = sem("consts_ready")
        ident_zero = sem("ident_zero")
        w_hi, w_lo = sem("w_hi"), sem("w_lo")
        stats_done, mv_done, var_done, rstd_done, xn_done = (sem(n) for n in (
            "stats_done", "mv_done", "var_done", "rstd_done", "xn_done"))
        first_ctx_hi, first_ctx_lo, ctx_split = sem("first_ctx_hi"), sem("first_ctx_lo"), sem("ctx_split")
        k_zeroed = sem("k_zeroed")
        xt_ready, xt_hi, xt_lo = sem("xt_ready"), sem("xt_hi"), sem("xt_lo")
        q_ready, q_hi, q_lo = sem("q_ready"), sem("q_hi"), sem("q_lo")
        k_ready, k_hi, k_lo = sem("k_ready"), sem("k_hi"), sem("k_lo")
        v_ready, v_copied = sem("v_ready"), sem("v_copied")

        def walk(eng, step):
            for u in range(2):
                step(u, u, 0, lambda d: u + d >= 0)
            with eng.Fori(1, NU // 2 - 1) as j:
                for s in range(2):
                    step(2 * j + s, s, j, lambda d: True)
            for u in range(NU - 2, NU - 1):
                step(u, u % 2, u // 2, lambda d: u + d < NU)

        block = stack.enter_context(nc.Block())

        @block.sync
        def _(sp):
            def load_unit(u, s):
                sp.dma_start(x1[:, bass.ds(UT * u, UT), :],
                             x[bass.ds(U * u, U), :].rearrange("(t p) d -> p t d", p=P)).then_inc(x_loaded[s], 16)

            def load_ctx(u, s):
                src = ctx_t[:, bass.ds(U * u, U)]
                sp.dma_start(ctx_raw[s][:, 0, :], src[0:P]).then_inc(ctx_loaded[s], 16)
                sp.dma_start(ctx_raw[s][0:REST, 1, :], src[P:C]).then_inc(ctx_loaded[s], 16)
                sp.dma_start(ctx_raw[s][REST:P, 1, :], src[P:C]).then_inc(ctx_loaded[s], 16)

            def store_unit(u, s):
                sp.wait_ge(k_hi, u + 1)
                sp.dma_start(k_dram[bass.ds(2 * u, 2), :, 0].rearrange("b e p t -> p (b e) t"),
                             k_h[s].rearrange("p b e t -> p (b e) t")).then_inc(k_stored[s], 16)
                sp.wait_ge(k_lo, 2 * u + 2)
                sp.dma_start(k_dram[bass.ds(2 * u, 2), :, 1].rearrange("b e p t -> p (b e) t"),
                             k_l[s].rearrange("p b e t -> p (b e) t")).then_inc(k_stored[s], 16)
                sp.wait_ge(q_hi, u + 1)
                sp.dma_start(q_dram[bass.ds(2 * u, 2), :, 0].rearrange("b e p t -> p (b e) t"),
                             q_h[s].rearrange("p b e t -> p (b e) t")).then_inc(q_stored[s], 16)
                sp.wait_ge(q_lo, 2 * u + 2)
                sp.dma_start(q_dram[bass.ds(2 * u, 2), :, 1].rearrange("b e p t -> p (b e) t"),
                             q_l[s].rearrange("p b e t -> p (b e) t")).then_inc(q_stored[s], 16)

            sp.dma_start(ctx_raw[0][:, 0, :], ctx_t[0:P, 0:U]).then_inc(first_loaded, 16)
            sp.dma_start(w_raw[2][:, 0, :], wk[0:P, :]).then_inc(first_loaded, 16)
            sp.dma_start(ctx_raw[0][0:REST, 1, :], ctx_t[P:C, 0:U]).then_inc(ctx_loaded[0], 16)
            sp.dma_start(ctx_raw[0][REST:P, 1, :], ctx_t[P:C, 0:U]).then_inc(ctx_loaded[0], 16)
            sp.dma_start(w_raw[2][0:REST, 1, :], wk[P:C, :]).then_inc(w_loaded[0], 16)
            sp.dma_start(w_raw[2][REST:P, 1, :], wk[P:C, :]).then_inc(w_loaded[0], 16)
            load_unit(0, 0)
            sp.dma_start(w_raw[3][:, 0, :], wv[0:P, :]).then_inc(w_loaded[1], 16)
            sp.dma_start(w_raw[3][0:REST, 1, :], wv[P:C, :]).then_inc(w_loaded[1], 16)
            sp.dma_start(w_raw[3][REST:P, 1, :], wv[P:C, :]).then_inc(w_loaded[1], 16)
            sp.dma_start(w_raw[0][:], wq.rearrange("(k p) n -> p k n", p=P)).then_inc(w_loaded[2], 16)
            load_ctx(1, 1)
            load_unit(1, 1)
            sp.dma_start(w_raw[1][:], wo.rearrange("(k p) n -> p k n", p=P)).then_inc(w_loaded[3], 16)
            sp.dma_start(bo_bc[:], bo.partition_broadcast(P)).then_inc(bo_loaded, 16)

            def step(u, s, turn, has):
                if has(2):
                    if isinstance(u, int) and u == 0:
                        sp.wait_ge(first_ctx_lo, 2)
                    else:
                        sp.wait_ge(ctx_split, 4 * u)
                    load_ctx(u + 2, s)
                if not has(2):
                    sp.wait_ge(k_stored[0], 32)
                    sp.wait_ge(q_stored[0], 32)
                    sp.wait_ge(q_zeroed, 1)
                    load_qk(sp, 0, 0, q_dram, k_dram, q_stack, k_stack, qk_loaded)
                store_unit(u, s)

            walk(sp, step)
            sp.wait_ge(bo_loaded, 16)

        @block.gpsimd
        def _(pool):
            nc.gpsimd.memset(ident[:], 0.0).then_inc(ident_zero, 1)
            pool.wait_ge(ident_zero, 1)
            nc.gpsimd.affine_select(out=ident[:], in_=ident[:], compare_op=ALU.not_equal, fill=1.0, base=0,
                                    pattern=[[-1, P]], channel_multiplier=1).then_inc(consts_ready, 1)
            nc.gpsimd.memset(half[:], -0.5).then_inc(consts_ready, 1)
            nc.gpsimd.memset(eps[:], EPS).then_inc(consts_ready, 1)
            pool.wait_ge(consts_ready, 3)

            for r in range(RING):
                nc.gpsimd.memset(v_pad[r][:, :, :, HD:HD + 1], 1.0)
                nc.gpsimd.memset(v_pad[r][:, :, :, HD + 1:32], 0.0)

            def rstd_unit(u, s):
                pool.wait_ge(mv_done, u + 1)
                if not (isinstance(u, int) and u == 0):
                    pool.wait_ge(rstd_done, u)
                nc.gpsimd.tensor_tensor(var_eps[:], mean_var[s][:, :, 1], eps[:], ALU.add).then_inc(var_done, 1)
                pool.wait_ge(var_done, u + 1)
                nc.gpsimd.tensor_tensor(rstd[s][:], var_eps[:], half[:], ALU.pow).then_inc(rstd_done, 1)

            def split_ctx(u, s):
                for k, rows in ((0, P), (1, REST)):
                    nc.gpsimd.tensor_copy(ctx_h[s][:, k, :], ctx_raw[s][:, k, :]).then_inc(ctx_split, 1)
                    pool.wait_ge(ctx_split, 4 * (u - 1) + 2 * k + 1)
                    nc.gpsimd.tensor_tensor(ctx_l[s][0:rows, k, :], ctx_raw[s][0:rows, k, :],
                                            ctx_h[s][0:rows, k, :], ALU.subtract).then_inc(ctx_split, 1)

            rstd_unit(0, 0)
            pool.wait_ge(ctx_loaded[1], 48)
            split_ctx(1, 1)
            rstd_unit(1, 1)

            def step(u, s, turn, has):
                if has(2):
                    pool.wait_ge(ctx_loaded[s], 48 * turn + (80 if s == 0 else 96))
                    pool.wait_ge(v_ready, u + 1)
                    rstd_unit(u + 2, s)
                    split_ctx(u + 2, s)
                zeroed = (0, 1) if not has(-1) else (2, 3) if not has(2) else ()
                if zeroed:
                    for r in zeroed:
                        nc.gpsimd.memset(q_stack[r][:].rearrange("p a t -> p (a t)").bitcast(I32), 0).then_inc(q_zeroed, 1)

            walk(pool, step)

        @block.vector
        def _(dve):
            def stats_unit(u, s, turn):
                dve.wait_ge(x_loaded[s], 16 * (turn + 1))
                if not early(u):
                    dve.wait_ge(mv_done, u - 1)
                    dve.wait_ge(xn_done, u - 1)
                    dve.wait_ge(rstd_done, u - 1)
                for t in range(UT):
                    last = nc.vector.bn_stats(stats[s][:, t, :], x1[:, bass.ds(UT * u + t, 1), :].rearrange("p a d -> p (a d)"))
                last.then_inc(stats_done, 1)

            def aggregate_unit(u, s):
                for t in range(UT):
                    last = nc.vector.bn_aggr(mean_var[s][:, t, :], stats[s][:, t, :])
                last.then_inc(mv_done, 1)

            def normalise_unit(u, s):
                dve.wait_ge(rstd_done, u + 1)
                if not early(u):
                    dve.wait_ge(xt_ready, u - 1)
                for t in range(UT):
                    last = nc.vector.tensor_scalar(xn[s][:, t, :], x1[:, bass.ds(UT * u + t, 1), :].rearrange("p a d -> p (a d)"),
                                                   mean_var[s][:, t, 0:1], rstd[s][:, t:t + 1],
                                                   ALU.subtract, ALU.mult)
                last.then_inc(xn_done, 1)

            def low(dst, ps, hi, scale, done):
                nc.vector.scalar_tensor_tensor(out=dst, in0=ps, scalar=scale, in1=hi,
                                               op0=ALU.mult, op1=ALU.subtract).then_inc(done, 1)

            def xt_low(u, s):
                dve.wait_ge(xt_hi, u + 1)
                low(xt_l[s][:], ps_x[:], xt_h[s][:], 1.0, xt_lo)

            def k_low(u, s, turn):
                dve.wait_ge(k_hi, u + 1)
                if not early(u):
                    dve.wait_ge(k_stored[s], 32 * turn)
                for e in range(2):
                    low(k_l[s][:, :, e], ps_k[:, e].rearrange("p (b t) -> p b t", b=2), k_h[s][:, :, e], 1.0 / WS, k_lo)

            def q_low(u, s, turn):
                dve.wait_ge(q_hi, u + 1)
                if not early(u):
                    dve.wait_ge(q_stored[s], 32 * turn)
                for e in range(2):
                    low(q_l[s][:, :, e], ps_q[:, e].rearrange("p (b t) -> p b t", b=2), q_h[s][:, :, e], SC / WS, q_lo)

            def weight_low(n):
                raw, hi, lo = ((w_raw[2], wk_h, wk_l), (w_raw[3], wv_h, wv_l), (w_raw[0], wq_h, wq_l), (w_raw[1], wo_h, wo_l))[n]
                dve.wait_ge(w_hi, 2 * n + 2)
                low(lo[:, 0, :], raw[:, 0, :], hi[:, 0, :], WS, w_lo)
                if n < 2:
                    low(hi[REST:P, 1, :], raw[REST:P, 1, :], hi[REST:P, 1, :], WS, w_lo)
                else:
                    low(lo[:, 1, :], raw[:, 1, :], hi[:, 1, :], WS, w_lo)

            for k, rows in ((0, P), (1, REST)):
                dve.wait_ge(first_ctx_hi, k + 1)
                nc.vector.tensor_tensor(ctx_l[0][0:rows, k, :], ctx_raw[0][0:rows, k, :], ctx_h[0][0:rows, k, :],
                                        ALU.subtract).then_inc(first_ctx_lo, 1)
                dve.wait_ge(w_hi, k + 1)
                if k == 0:
                    low(wk_l[:, 0, :], w_raw[2][:, 0, :], wk_h[:, 0, :], WS, w_lo)
                else:
                    low(wk_h[REST:P, 1, :], w_raw[2][REST:P, 1, :], wk_h[REST:P, 1, :], WS, w_lo)
            stats_unit(0, 0, 0)
            dve.wait_ge(stats_done, 1)
            aggregate_unit(0, 0)
            weight_low(1)
            weight_low(2)
            normalise_unit(0, 0)
            stats_unit(1, 1, 0)
            dve.wait_ge(stats_done, 2)
            aggregate_unit(1, 1)

            def first_step():
                k_low(0, 0, 0)
                xt_low(0, 0)
                stats_unit(2, 0, 1)
                dve.wait_ge(stats_done, 3)
                normalise_unit(1, 1)
                aggregate_unit(2, 0)
                q_low(0, 0, 0)
                xt_low(1, 1)
                weight_low(3)

            def step(u, s, turn, has):
                if not has(-1):
                    first_step()
                    return
                if has(1):
                    normalise_unit(u + 1, 1 - s)
                k_low(u, s, turn)
                if has(2):
                    stats_unit(u + 2, s, turn + 1)
                    dve.wait_ge(stats_done, u + 3)
                q_low(u, s, turn)
                if has(2):
                    aggregate_unit(u + 2, s)
                if has(1):
                    xt_low(u + 1, 1 - s)

            walk(dve, step)

        @block.scalar
        def _(act):
            def xt_high(u, s):
                act.wait_ge(xt_ready, u + 1)
                if not early(u):
                    act.wait_ge(q_ready, u - 1)
                nc.scalar.activation(xt_h[s][:], ps_x[:], ACT.Copy).then_inc(xt_hi, 1)

            def k_high(u, s, turn):
                act.wait_ge(k_ready, u + 1)
                if not early(u):
                    act.wait_ge(k_stored[s], 32 * turn)
                nc.scalar.activation(k_h[s].rearrange("p b e t -> p e b t"),
                                     ps_k[:].rearrange("p e (b t) -> p e b t", b=2), ACT.Copy, scale=1.0 / WS).then_inc(k_hi, 1)

            def q_high(u, s, turn):
                act.wait_ge(q_ready, u + 1)
                if not early(u):
                    act.wait_ge(q_stored[s], 32 * turn)
                nc.scalar.activation(q_h[s].rearrange("p b e t -> p e b t"),
                                     ps_q[:].rearrange("p e (b t) -> p e b t", b=2), ACT.Copy, scale=SC / WS).then_inc(q_hi, 1)

            def v_copy(u):
                act.wait_ge(v_ready, u + 1)
                nc.scalar.activation(v_all[:, bass.ds(UT * u, UT), :].rearrange("p t n -> p (t n)"),
                                     ps_v[:].rearrange("p a b -> p (a b)"), ACT.Copy, scale=1.0 / WS).then_inc(v_copied, 1)

            def weight_high(n):
                raw, hi = ((w_raw[2], wk_h), (w_raw[3], wv_h), (w_raw[0], wq_h), (w_raw[1], wo_h))[n]
                act.wait_ge(w_loaded[n], 48 if n == 1 else 16)
                nc.scalar.activation(hi[:, 0, :], raw[:, 0, :], ACT.Copy, scale=WS).then_inc(w_hi, 1)
                nc.scalar.activation(hi[:, 1, :], raw[:, 1, :], ACT.Copy, scale=WS).then_inc(w_hi, 1)

            def zero_k(r):
                nc.scalar.activation(k_stack[r][:].rearrange("p a e t -> p (a e t)").bitcast(F32),
                                     ident[:, 0:1].to_broadcast([P, PAIRS * N]), ACT.Copy, scale=0.0).then_inc(k_zeroed, 1)

            act.wait_ge(consts_ready, 3)
            zero_k(0)
            def first_ctx_high(k):
                nc.scalar.activation(ctx_h[0][:, k, :], ctx_raw[0][:, k, :], ACT.Copy).then_inc(first_ctx_hi, 1)

            act.wait_ge(first_loaded, 32)
            first_ctx_high(0)
            nc.scalar.activation(wk_h[:, 0, :], w_raw[2][:, 0, :], ACT.Copy, scale=WS).then_inc(w_hi, 1)
            act.wait_ge(ctx_loaded[0], 32)
            first_ctx_high(1)
            act.wait_ge(w_loaded[0], 32)
            nc.scalar.activation(wk_h[:, 1, :], w_raw[2][:, 1, :], ACT.Copy, scale=WS).then_inc(w_hi, 1)
            weight_high(1)
            weight_high(2)

            def step(u, s, turn, has):
                if has(2):
                    act.wait_ge(x_loaded[s], 16 * turn + 16)
                    act.dma_start(x1[:, bass.ds(UT * (u + 2), UT), :],
                                  x[bass.ds(U * (u + 2), U), :].rearrange("(t p) d -> p t d", p=P)).then_inc(x_loaded[s], 16)
                k_high(u, s, turn)
                if not has(2):
                    zero_k(3)
                if not has(-1):
                    xt_high(0, 0)
                    v_copy(0)
                q_high(u, s, turn)
                if has(1):
                    xt_high(u + 1, 1 - s)
                if has(-1):
                    v_copy(u)
                else:
                    weight_high(3)
                if not has(-2):
                    zero_k(u + 1)

            walk(act, step)

        @block.tensor
        def _(pe):
            def transpose_x(u, s, first):
                pe.wait_ge(xn_done, u + 1)
                if not first:
                    pe.wait_ge(xt_lo, u)
                for k in range(DK):
                    for t in range(UT):
                        last = nc.tensor.transpose(ps_x[:, k, P * t:P * (t + 1)], xn[s][:, t, P * k:P * (k + 1)], ident[:])
                last.then_inc(xt_ready, 1)

            def project_q(u, s, first):
                pe.wait_ge(xt_lo, u + 1)
                if not first:
                    pe.wait_ge(q_lo, 2 * u)
                for e in range(2):
                    cols = slice(P * e, P * (e + 1))
                    for n, (w, v) in enumerate(((wq_h, xt_h), (wq_l, xt_h), (wq_h, xt_l))):
                        for k in range(DK):
                            last = nc.tensor.matmul(ps_q[:, e, :], w[:, k, cols], v[s][:, k, :],
                                                    start=(n + k == 0), stop=(n == 2 and k == DK - 1))
                last.then_inc(q_ready, 1)

            def project_k(u, s, first):
                if first:
                    pe.wait_ge(first_ctx_lo, 1)
                    pe.wait_ge(w_lo, 1)
                else:
                    pe.wait_ge(ctx_split, 4 * u)
                    pe.wait_ge(k_lo, 2 * u)
                for e in range(2):
                    cols = slice(P * e, P * (e + 1))
                    for n, (w, v, k, rows) in enumerate(ctx_terms(wk_h, wk_l, ctx_h[s], ctx_l[s])):
                        if first and e == 0 and n == 3:
                            pe.wait_ge(first_ctx_lo, 2)
                            pe.wait_ge(w_lo, 2)
                        last = nc.tensor.matmul(ps_k[:, e, :], w[0:rows, k, cols], v[0:rows, k, :],
                                                start=(n == 0), stop=(n == CTX_TERMS - 1))
                last.then_inc(k_ready, 1)

            def project_v(u, s, first):
                if not first:
                    pe.wait_ge(v_copied, u)
                for t in range(UT):
                    for n, (w, v, k, rows) in enumerate(ctx_terms(wv_h, wv_l, ctx_h[s], ctx_l[s])):
                        last = nc.tensor.matmul(ps_v[:, t // 2, D * (t % 2):D * (t % 2 + 1)],
                                                v[0:rows, k, P * t:P * (t + 1)], w[0:rows, k, :],
                                                start=(n == 0), stop=(n == CTX_TERMS - 1))
                last.then_inc(v_ready, 1)

            def step(u, s, turn, has):
                project_k(u, s, not has(-1))
                if not has(-1):
                    pe.wait_ge(consts_ready, 3)
                    transpose_x(0, 0, True)
                    pe.wait_ge(w_lo, 4)
                    project_v(0, 0, True)
                    pe.wait_ge(w_lo, 6)
                project_q(u, s, not has(-1))
                if has(1):
                    transpose_x(u + 1, 1 - s, False)
                if has(-1):
                    project_v(u, s, False)

            walk(pe, step)


def attend_and_feed(nc, x1, ident, bo_bc, wo_h, wo_l, q_dram, k_dram, v_all, q_stack, k_stack, v_pad,
                    wg, wu, wd, w16, w_large, out, half, eps, norm_buffers, late, w_split, ctx_odd, qk_odd,
                    q_stored, k_stored, qk_loaded):
    stack = ExitStack()
    with stack:
        def sb(name, shape, dt):
            return stack.enter_context(nc.sbuf_tensor(name, shape, dt))

        def sem(name):
            return stack.enter_context(nc.semaphore(name))

        probs = [sb(f"probs{i}", [P, 2, 2, 2, N], F32) for i in range(2)]
        diag = sb("diag", [2, 2, N], F16)
        neg_max = [sb(f"neg_max{i}", [P, P], F32) for i in range(2)]
        max_t = [sb(f"max_t{i}", [2 * H, P], F16) for i in range(2)]
        o_t = sb("o_t", [P, GROUPS, N], F32)
        rsum = [sb(f"rsum{i}", [P, H], F32) for i in range(2)]
        o_n = [sb(f"o_n{i}", [P, H, HD], F32) for i in range(2)]
        ot_h = sb("ot_h", [P, DK, N], F16)
        ot_l = sb("ot_l", [P, DK, N], F16)

        ps_s = [stack.enter_context(nc.psum_tensor(f"ps_s{i}", [P, 2, 2, N], F32)) for i in range(2)]
        ps_ms = stack.enter_context(nc.psum_tensor("ps_ms", [P, 2, 2, N], F32))
        ps_oc = stack.enter_context(nc.psum_tensor("ps_oc", [P, 2, 2 * N], F32))
        ps_m = [ps_ms[:, h] for h in range(2)]
        ps_o, ps_c = ps_oc[:, 0], ps_oc[:, 1]

        w_max = sb("w_max", [P, 4], F32)
        w_top = sb("w_top", [P, 1], F32)
        w_loaded = [sem(f"w_loaded{n}") for n in range(2)]
        w32_loaded, w32_made = [sem(f"w32_loaded{n}") for n in range(3)], sem("w32_made")
        w_made, w_max_done, w_flag = sem("w_made"), sem("w_max_done"), sem("w_flag")
        max_loaded = [sem(f"max_loaded{i}") for i in range(RING)]
        max_cleared, v_padded, bo_added = sem("max_cleared"), sem("v_padded"), sem("bo_added")
        diag_made, ones_loaded = sem("diag_made"), sem("ones_loaded")
        half_scored, half_reduced = sem("half_scored"), sem("half_reduced")
        max_transposed, max_copied = sem("max_transposed"), sem("max_copied")
        pair_scored, pair_exp = sem("pair_scored"), sem("pair_exp")
        pv_ready, pv_copied = sem("pv_ready"), sem("pv_copied")
        back_ready, recip_done, normed = sem("back_ready"), sem("recip_done"), sem("normed")
        ot_ready, ot_hi, ot_lo = sem("ot_ready"), sem("ot_hi"), sem("ot_lo")
        wo_ready, res_done = sem("wo_ready"), sem("res_done")

        LOOPS = 3

        def walk_batches(eng, start, step):
            for i in range(start):
                step(i, i, lambda d: (i + d) // RING, lambda d: i + d >= 0)
            with eng.Fori(0, LOOPS) as j:
                for k in range(start, start + RING):
                    step(RING * j + k, k, lambda d: j + (k + d) // RING, lambda d: True)
            for i in range(start + LOOPS * RING, B):
                step(i, i, lambda d: (i + d) // RING, lambda d: i + d < B)

        wq_h, wq_l, wk_h, wk_l, wv_h, wv_l = w_split
        last_ctx_h, last_ctx_l = ctx_odd
        last_q_h, last_q_l, last_k_h, last_k_l = qk_odd
        last_v_ready, last_v_copied = sem("last_v_ready"), sem("last_v_copied")
        last_k_ready, last_k_hi, last_k_lo = sem("last_k_ready"), sem("last_k_hi"), sem("last_k_lo")
        last_q_ready, last_q_hi, last_q_lo = sem("last_q_ready"), sem("last_q_hi"), sem("last_q_lo")

        stats, mean_var, rstd, var_eps, xn, xt_h, xt_l = norm_buffers
        last_xt_h, last_xt_l = xt_h[1], xt_l[1]

        def w_chunk(c):
            parts, cols = w16[c // 2].shape[1] // 2, w16[c // 2].shape[2]
            return xn[c % 2][:].rearrange("p t d -> p (t d)")[:, 0:parts * cols].bitcast(I32).rearrange("p (k n) -> p k n", k=parts)

        assert (B - 4) % RING == 0
        w32 = [k_stack[n][:].rearrange("p a e t -> p (a e t)").bitcast(F32)[:, 0:DK * FF]
               .rearrange("p (k n) -> p k n", n=w16[n].shape[2]) for n in range(3)]

        silu = [sb(f"feed_silu{i}", [P, U], F32) for i in range(2)]
        assert 2 * FT * U + 2 * DK * U <= TILES * D
        v_flat = v_all[:].rearrange("p t n -> p (t n)")
        hid_f = [v_flat[:, FT * U * i:FT * U * (i + 1)].rearrange("p (f t) -> p f t", f=FT) for i in range(2)]
        xt_f = [v_flat[:, 2 * FT * U + DK * U * i:2 * FT * U + DK * U * (i + 1)].rearrange("p (k t) -> p k t", k=DK)
                for i in range(2)]
        hid_h = [late[:, FT * U * i:FT * U * (i + 1)].rearrange("p (f t) -> p f t", f=FT) for i in range(2)]
        hid_l = [late[:, 2 * FT * U:].rearrange("p (f t) -> p f t", f=FT),
                 probs[1][:].rearrange("p a e k q -> p (a e k q)")[:, 0:FT * U // 2].bitcast(F16)
                 .rearrange("p (f t) -> p f t", f=FT)]

        ps_x = ps_ms[:].rearrange("p e h k -> p e (h k)")
        ps_g = [ps_s[i][:, 0].rearrange("p k q -> p (k q)") for i in range(2)]
        ps_u = [ps_s[i][:, 1].rearrange("p k q -> p (k q)") for i in range(2)]
        ps_y = ps_oc[:].rearrange("p a (t d) -> p (a t) d", t=2)

        stats_done, mv_done, var_done, rstd_done, xn_done = (sem("feed_" + n) for n in (
            "stats_done", "mv_done", "var_done", "rstd_done", "xn_done"))
        xt_ready, xt_full, xt_hi, xt_lo = sem("feed_xt_ready"), sem("feed_xt_full"), sem("feed_xt_hi"), sem("feed_xt_lo")
        gu_ready, silu_done, hid_done, hid_hi, hid_lo = (sem("feed_" + n) for n in (
            "gu_ready", "silu_done", "hid_done", "hid_hi", "hid_lo"))
        y_ready, y_done = sem("feed_y_ready"), sem("feed_y_done")
        stored = [sem(f"feed_stored{i}") for i in range(2)]

        def walk_units(eng, step):
            for u in range(2):
                step(u, u % 2, lambda d: u + d >= 0)
            with eng.Fori(1, NU // 2 - 1) as j:
                for s in range(2):
                    step(2 * j + s, s, lambda d: True)
            for u in range(NU - 2, NU):
                step(u, u % 2, lambda d: u + d < NU)

        block = stack.enter_context(nc.Block())

        @block.sync
        def _(sp):
            def load_max(b, r):
                sp.wait_ge(max_copied, b + 1)
                sp.dma_start(q_stack[r][ROW_MAX:ROW_MAX + 2, :, :], max_t[r % 2][:]).then_inc(max_loaded[r], 16)

            def load_w_chunk(c):
                w, parts = (wg, wu, wd)[c // 2], w16[c // 2].shape[1] // 2
                if c >= 2:
                    sp.wait_ge(w_made, c - 1)
                sp.dma_start(w_chunk(c), w.rearrange("(k p) n -> p k n", p=P)[:, parts * (c % 2):parts * (c % 2 + 1)]).then_inc(w_loaded[c % 2], 16)

            def step(i, r, turn, has):
                if has(3) and has(-1):
                    sp.wait_ge(pair_scored, PAIRS * i)
                    load_qk(sp, i + 3, (r + 3) % RING, q_dram, k_dram, q_stack, k_stack, qk_loaded)
                if has(1):
                    load_max(i + 1, (r + 1) % RING)
                if not has(3):
                    n = i - (B - 3)
                    sp.wait_ge(pair_scored, PAIRS * i)
                    sp.dma_start(w32[n].bitcast(I32), (wg, wu, wd)[n].rearrange("(k p) n -> p k n", p=P)).then_inc(w32_loaded[n], 16)
                if not has(-1):
                    for c in range(2, 6):
                        load_w_chunk(c)

            load_qk(sp, 1, 1, q_dram, k_dram, q_stack, k_stack, qk_loaded)
            sp.wait_ge(k_stored[1], 32)
            sp.wait_ge(q_stored[1], 32)
            load_qk(sp, 2, 2, q_dram, k_dram, q_stack, k_stack, qk_loaded)
            sp.wait_ge(diag_made, 1)
            for r in range(RING):
                sp.dma_start(k_stack[r][ROW_MAX:ROW_MAX + 2].rearrange("r p e t -> r p (e t)"),
                             diag[:].rearrange("r e t -> r (e t)").unsqueeze(1).to_broadcast([2, PAIRS, 2 * N])).then_inc(ones_loaded, 16)
            last = bass.ds(B - 2, 2)
            sp.wait_ge(last_k_hi, 2)
            sp.dma_start(k_dram[last, :, 0].rearrange("b e p t -> p (b e) t"),
                         last_k_h.rearrange("p b e t -> p (b e) t")).then_inc(k_stored[1], 16)
            sp.wait_ge(last_k_lo, 2)
            sp.dma_start(k_dram[last, :, 1].rearrange("b e p t -> p (b e) t"),
                         last_k_l.rearrange("p b e t -> p (b e) t")).then_inc(k_stored[1], 16)
            load_max(0, 0)
            sp.wait_ge(last_q_hi, 2)
            sp.dma_start(q_dram[last, :, 0].rearrange("b e p t -> p (b e) t"),
                         last_q_h.rearrange("p b e t -> p (b e) t")).then_inc(q_stored[1], 16)
            sp.wait_ge(last_q_lo, 2)
            sp.dma_start(q_dram[last, :, 1].rearrange("b e p t -> p (b e) t"),
                         last_q_l.rearrange("p b e t -> p (b e) t")).then_inc(q_stored[1], 16)
            load_qk(sp, 3, 3, q_dram, k_dram, q_stack, k_stack, qk_loaded)
            load_w_chunk(0)
            load_w_chunk(1)
            for s in range(2):
                sp.wait_ge(q_stored[s], 32 * NU // 2)
                sp.wait_ge(k_stored[s], 32 * NU // 2)
            walk_batches(sp, 1, step)
            for r in range(RING):
                sp.wait_ge(qk_loaded[r], 16 * QK_DMAS * B // RING)
                sp.wait_ge(max_loaded[r], 16 * B // RING)

            def unit_step(u, s, has):
                if has(1):
                    sp.wait_ge(y_done, u + 1)
                    sp.dma_start(out[bass.ds(U * u, U), :].rearrange("(t p) d -> p t d", p=P),
                                 x1[:, bass.ds(UT * u, UT), :]).then_inc(stored[s], 16)
                else:
                    for h in range(2):
                        sp.wait_ge(y_done, NU + h)
                        rows = bass.ds(U * u + U // 2 * h, U // 2)
                        sp.dma_start(out[rows, :].rearrange("(t p) d -> p t d", p=P),
                                     x1[:, UT * u + 2 * h:UT * u + 2 * h + 2, :]).then_inc(stored[s], 16)

            walk_units(sp, unit_step)
            sp.wait_ge(stored[0], 16 * NU // 2)
            sp.wait_ge(stored[1], 16 * NU // 2 + 16)

        @block.gpsimd
        def _(pool):
            def pad_v(b, r):
                nc.gpsimd.tensor_copy(v_pad[r][:, :, :, 0:HD],
                                      v_all[:, bass.ds(2 * b, 2), :].rearrange("p t (h d) -> p t h d", h=H)).then_inc(v_padded, 1)

            def add_bo(b):
                for t in range(2):
                    tile = x1[:, bass.ds(2 * b + t, 1), :].rearrange("p a d -> p (a d)")
                    nc.gpsimd.tensor_tensor(tile, tile, bo_bc[:], ALU.add).then_inc(bo_added, 1)

            def weight_to_float(n):
                pool.wait_ge(w32_loaded[n], 16)
                nc.gpsimd.tensor_copy(w32[n], w32[n].bitcast(I32)).then_inc(w32_made, 1)

            def step(i, r, turn, has):
                if has(3) and has(-1):
                    pool.wait_ge(pv_ready, GROUPS * i)
                if has(2):
                    add_bo(i + 2)
                if has(3):
                    pad_v(i + 3, (r + 3) % RING)
                elif has(2):
                    weight_to_float(0)

            for n in range(2):
                nc.gpsimd.memset(neg_max[n][:], 0.0).then_inc(max_cleared, 1)
            for b in range(3):
                pad_v(b, b)
            for b in range(2):
                add_bo(b)
            pool.wait_ge(last_v_copied, 2)
            for c in range(6):
                parts = w16[c // 2].shape[1] // 2
                pool.wait_ge(w_loaded[c % 2], 16 * (c // 2 + 1))
                nc.gpsimd.tensor_copy(w16[c // 2][:, parts * (c % 2):parts * (c % 2 + 1), :], w_chunk(c)).then_inc(w_made, 1)
            walk_batches(pool, 1, step)
            pool.wait_ge(w_max_done, 4)
            nc.gpsimd.partition_all_reduce(w_top[:], w_max[:, 3:4], P, bass.bass_isa.ReduceOp.max).then_inc(w_flag, 1)
            pool.wait_ge(w_flag, 1)
            nc.gpsimd.tensor_scalar(w_large[:], w_top[:], INT_EXACT, None, ALU.is_ge).then_inc(w_flag, 1)
            pool.wait_ge(w_flag, 2)

            def rstd_unit(u, s):
                pool.wait_ge(mv_done, u + 1)
                nc.gpsimd.tensor_tensor(var_eps[:], mean_var[s][:, :, 1], eps[:], ALU.add).then_inc(var_done, 1)
                pool.wait_ge(var_done, u + 1)
                nc.gpsimd.tensor_tensor(rstd[s][:], var_eps[:], half[:], ALU.pow).then_inc(rstd_done, 1)
                pool.wait_ge(rstd_done, u + 1)

            def unit_step(u, s, has):
                if has(2):
                    rstd_unit(u + 2, s)

            rstd_unit(0, 0)
            rstd_unit(1, 1)
            weight_to_float(1)
            weight_to_float(2)
            walk_units(pool, unit_step)

        @block.vector
        def _(dve):
            def reduce_pair(b, r, p, first):
                cols = neg_max[r % 2][:, 0:2 * H].rearrange("q (e p h) -> q p h e", e=2, p=PAIRS)
                for h in range(2):
                    dve.wait_ge(half_scored, H * b + 2 * p + h + 1)
                    if p == 0 and h == 0 and not first:
                        dve.wait_ge(max_transposed, b - 1)
                    nc.vector.tensor_reduce(cols[:, p, h], ps_m[h], AXX, ALU.max,
                                            negate=True).then_inc(half_reduced, 1)

            def normalise(b, h):
                dve.wait_ge(back_ready, 2 * b + h + 1)
                dve.wait_ge(normed, 2 * b)
                heads = ps_c.rearrange("p (h c) -> p h c", h=H)
                nc.vector.reciprocal(rsum[h][:], heads[:, :, HD]).then_inc(recip_done, 1)
                dve.wait_ge(recip_done, 2 * b + h + 1)
                dve.wait_ge(ot_ready, b)
                nc.vector.tensor_tensor(o_n[h][:], heads[:, :, 0:HD],
                                        rsum[h][:].unsqueeze(2).to_broadcast([P, H, HD]), ALU.mult).then_inc(normed, 1)

            def ot_low(b):
                dve.wait_ge(ot_hi, b + 1)
                nc.vector.tensor_tensor(ot_l[:].rearrange("p k t -> p (k t)"), ps_c,
                                        ot_h[:].rearrange("p k t -> p (k t)"), ALU.subtract).then_inc(ot_lo, 1)

            def residual_attn(b):
                dve.wait_ge(wo_ready, b + 1)
                dve.wait_ge(bo_added, 2 * b + 2)
                tiles = x1[:, bass.ds(2 * b, 2), :].rearrange("p t d -> p (t d)")
                nc.vector.scalar_tensor_tensor(out=tiles, in0=ps_c, scalar=1.0 / WS, in1=tiles,
                                               op0=ALU.mult, op1=ALU.add).then_inc(res_done, 1)

            def step(i, r, turn, has):
                for p in range(PAIRS):
                    if 4 <= p < 7 and has(1) and not has(2):
                        dve.wait_ge(w_made, 2 * (p - 4) + 2)
                        w = w16[p - 4][:]
                        nc.vector.tensor_reduce(w_max[:, p - 4:p - 3], w.rearrange("p k n -> p (k n)"), AXX, ALU.max,
                                                apply_absolute_value=True).then_inc(w_max_done, 1)
                    if p == 7 and has(1) and not has(2):
                        dve.wait_ge(w_max_done, 3)
                        nc.vector.tensor_reduce(w_max[:, 3:4], w_max[:, 0:3], AXX, ALU.max).then_inc(w_max_done, 1)
                    if p < 4 and has(1):
                        reduce_pair(i + 1, (r + 1) % RING, p + 4, False)
                    if p >= 4 and has(2):
                        reduce_pair(i + 2, (r + 2) % RING, p - 4, False)
                    if has(-1):
                        if p in (1, 2):
                            normalise(i - 1, p - 1)
                        if p == 4:
                            ot_low(i - 1)
                        if p == 7:
                            residual_attn(i - 1)
                    if not has(1):
                        if p == 0:
                            stats_unit(0, 0, True)
                        if p == 1:
                            dve.wait_ge(stats_done, 1)
                            aggregate_unit(0, 0)
                        if p == 3:
                            normalise_unit(0, 0, True)
                        if p == 5:
                            stats_unit(1, 1, True)
                        if p == 6:
                            dve.wait_ge(stats_done, 2)
                            aggregate_unit(1, 1)
                            xt_low(0, 0)
                        if p == 7:
                            normalise_unit(1, 1, True)

            def stats_unit(u, s, first):
                if not first:
                    dve.wait_ge(mv_done, u - 1)
                    dve.wait_ge(xn_done, u - 1)
                    dve.wait_ge(rstd_done, u - 1)
                for t in range(UT):
                    last = nc.vector.bn_stats(stats[s][:, t, :], x1[:, bass.ds(UT * u + t, 1), :].rearrange("p a d -> p (a d)"))
                last.then_inc(stats_done, 1)

            def aggregate_unit(u, s):
                for t in range(UT):
                    last = nc.vector.bn_aggr(mean_var[s][:, t, :], stats[s][:, t, :])
                last.then_inc(mv_done, 1)

            def normalise_unit(u, s, first):
                dve.wait_ge(rstd_done, u + 1)
                if not first:
                    dve.wait_ge(xt_ready, u - 1)
                for t in range(UT):
                    last = nc.vector.tensor_scalar(xn[s][:, t, :], x1[:, bass.ds(UT * u + t, 1), :].rearrange("p a d -> p (a d)"),
                                                   mean_var[s][:, t, 0:1], rstd[s][:, t:t + 1],
                                                   ALU.subtract, ALU.mult)
                last.then_inc(xn_done, 1)

            def xt_low(u, s):
                dve.wait_ge(xt_hi, u + 1)
                nc.vector.tensor_tensor(xt_l[s][:], ps_x, xt_h[s][:], ALU.subtract).then_inc(xt_lo, 1)

            def hidden(u, s, f, first):
                dve.wait_ge(silu_done, FT * u + f + 1)
                if f == 0 and first:
                    dve.wait_ge(v_padded, B)
                if f == 0 and not first:
                    dve.wait_ge(y_ready, u - 1)
                    dve.wait_ge(hid_hi, FT * (u - 1))
                nc.vector.scalar_tensor_tensor(out=hid_f[s][:, f, :], in0=ps_u[f % 2], scalar=W_SCALE * HS,
                                               in1=silu[f % 2][:], op0=ALU.mult, op1=ALU.mult).then_inc(hid_done, 1)

            def hidden_low(u, s, f):
                dve.wait_ge(hid_hi, FT * u + f + 1)
                nc.vector.tensor_tensor(hid_l[s][:, f, :], hid_f[s][:, f, :], hid_h[s][:, f, :],
                                        ALU.subtract).then_inc(hid_lo, 1)

            def residual_ff(u):
                dve.wait_ge(y_ready, u + 1)
                tiles = x1[:, bass.ds(UT * u, UT), :].rearrange("p t d -> p (t d)")
                nc.vector.scalar_tensor_tensor(out=tiles, in0=ps_y.rearrange("p t d -> p (t d)"),
                                               scalar=W_SCALE / HS, in1=tiles,
                                               op0=ALU.mult, op1=ALU.add).then_inc(y_done, 1)

            def unit_step(u, s, has):
                for f in range(FT):
                    early_low = f == FT - 1 and not has(1)
                    if early_low:
                        hidden_low(u, s, f - 1)
                    hidden(u, s, f, not has(-2))
                    if not has(-1):
                        if f == 0:
                            stats_unit(2, s, False)
                            dve.wait_ge(stats_done, 3)
                            aggregate_unit(2, s)
                        if f in (1, 2):
                            normalise(B - 1, f - 1)
                        if f == 4:
                            ot_low(B - 1)
                        if f == 5:
                            residual_attn(B - 1)
                    if f == 0 and has(1) and has(-1):
                        normalise_unit(u + 1, 1 - s, False)
                    if f > 0 and not early_low:
                        hidden_low(u, s, f - 1)
                    if f == 3:
                        if has(1):
                            xt_low(u + 1, 1 - s)
                        if has(2) and has(-1):
                            stats_unit(u + 2, s, False)
                            dve.wait_ge(stats_done, u + 3)
                        if has(-1):
                            residual_ff(u - 1)
                        if has(2) and has(-1):
                            aggregate_unit(u + 2, s)
                hidden_low(u, s, FT - 1)

            def last_low(e, ps, hi, lo, scale, high, low):
                dve.wait_ge(high, e + 1)
                nc.vector.scalar_tensor_tensor(out=lo[:, :, e], in0=ps[:, e], scalar=scale,
                                               in1=hi[:, :, e], op0=ALU.mult, op1=ALU.subtract).then_inc(low, 1)

            nc.vector.tensor_copy(diag[:], ident[0:2, 0:2].unsqueeze(2).to_broadcast([2, 2, N])).then_inc(diag_made, 1)
            dve.wait_ge(max_cleared, 2)
            for n in range(PAIRS + 4):
                reduce_pair(n // PAIRS, n // PAIRS, n % PAIRS, True)
                if n in (1, 3):
                    last_low((n - 1) // 2, ps_s[0], last_k_h, last_k_l, 1.0 / WS, last_k_hi, last_k_lo)
                if n in (5, 7):
                    last_low((n - 5) // 2, ps_s[1], last_q_h, last_q_l, SC / WS, last_q_hi, last_q_lo)
            walk_batches(dve, 2, step)

            walk_units(dve, unit_step)
            for h in range(2):
                dve.wait_ge(y_ready, NU + h)
                tiles = x1[:, TILES - 4 + 2 * h:TILES - 2 + 2 * h, :].rearrange("p t d -> p (t d)")
                nc.vector.scalar_tensor_tensor(out=tiles, in0=ps_y[:, 2 * h:2 * h + 2, :].rearrange("p t d -> p (t d)"),
                                               scalar=W_SCALE / HS, in1=tiles,
                                               op0=ALU.mult, op1=ALU.add).then_inc(y_done, 1)

        @block.scalar
        def _(act):
            def exp_pair(b, p, first):
                g = p // 2
                act.wait_ge(pair_scored, PAIRS * b + p + 1)
                if p % 2 == 0 and not (first and g < 2):
                    act.wait_ge(pv_ready, GROUPS * b + g - 1)
                nc.scalar.activation(probs[g % 2][:, p % 2].rearrange("p e k q -> p (e k q)"),
                                     ps_s[p % 2][:].rearrange("p e k q -> p (e k q)"), ACT.Exp).then_inc(pair_exp, 1)

            def copy_pv(b, g, first):
                act.wait_ge(pv_ready, GROUPS * b + g + 1)
                if g == 0 and not first:
                    act.wait_ge(back_ready, 2 * b)
                nc.scalar.activation(o_t[:, g, :], ps_o[:, 0:N], ACT.Copy).then_inc(pv_copied, 1)

            def ot_high(b, first):
                act.wait_ge(ot_ready, b + 1)
                if not first:
                    act.wait_ge(wo_ready, b)
                nc.scalar.activation(ot_h[:].rearrange("p k t -> p (k t)"), ps_c, ACT.Copy).then_inc(ot_hi, 1)

            def copy_max(b, r, turn):
                act.wait_ge(max_transposed, b + 1)
                if turn is not None:
                    act.wait_ge(max_loaded[(r + 2) % RING], 16 * turn)
                nc.scalar.activation(max_t[r % 2][:], ps_o[0:2 * H, N:N + P], ACT.Copy).then_inc(max_copied, 1)

            def step(i, r, turn, has):
                for p in range(PAIRS):
                    if p == 0 and has(-1):
                        copy_pv(i - 1, 3, False)
                    if has(0):
                        exp_pair(i, p, not has(-1))
                        if p in (2, 4, 6):
                            copy_pv(i, p // 2 - 1, not has(-1))
                    if p == 3 and has(-1):
                        ot_high(i - 1, not has(-2))
                    if p == 4 and has(1):
                        copy_max(i + 1, (r + 1) % RING, turn(-1) + 1 if has(-1) else None)
                    if p == 5 and not has(1):
                        first_xt_high()

            def xt_copies(u, s, first):
                act.wait_ge(xt_ready, u + 1)
                if not first:
                    act.wait_ge(gu_ready, FT * (u - 1))
                nc.scalar.activation(xt_f[s][:], ps_x, ACT.Copy).then_inc(xt_full, 1)
                nc.scalar.activation(xt_h[s][:], ps_x, ACT.Copy).then_inc(xt_hi, 1)

            def first_xt_high():
                act.wait_ge(xt_ready, 1)
                nc.scalar.activation(xt_h[0][:], ps_x, ACT.Copy).then_inc(xt_hi, 1)

            def first_xt_whole():
                act.wait_ge(v_padded, B)
                act.wait_ge(xt_lo, 1)
                nc.scalar.activation(xt_f[0][:], ps_x, ACT.Copy).then_inc(xt_full, 1)

            def gate_silu(u, f, first):
                act.wait_ge(gu_ready, FT * u + f + 1)
                if not (first and f < 2):
                    act.wait_ge(hid_done, FT * u + f - 1)
                nc.scalar.activation(silu[f % 2][:], ps_g[f % 2], ACT.Silu, scale=W_SCALE).then_inc(silu_done, 1)

            def hidden_high(u, s, f, first):
                act.wait_ge(hid_done, FT * u + f + 1)
                if f == 0 and not first:
                    act.wait_ge(y_ready, u - 1)
                    act.wait_ge(hid_lo, FT * (u - 1))
                nc.scalar.activation(hid_h[s][:, f, :], hid_f[s][:, f, :], ACT.Copy).then_inc(hid_hi, 1)

            def unit_step(u, s, has):
                for f in range(FT):
                    early_high = f == FT - 1 and not has(1)
                    if early_high:
                        hidden_high(u, s, f - 1, False)
                    gate_silu(u, f, not has(-1))
                    if f == 0 and not has(-1):
                        copy_pv(B - 1, GROUPS - 1, False)
                    if f == 4 and not has(-1):
                        ot_high(B - 1, False)
                    if f > 0 and not early_high:
                        hidden_high(u, s, f - 1, not has(-2))
                    if f == 2 and has(1):
                        xt_copies(u + 1, 1 - s, not has(-1))
                hidden_high(u, s, FT - 1, False)

            def last_high(e, ps, hi, scale, ready, high):
                act.wait_ge(ready, e + 1)
                nc.scalar.activation(hi[:, :, e], ps[:, e], ACT.Copy, scale=scale).then_inc(high, 1)

            act.wait_ge(k_stored[1], 32 * (NU // 2 - 1))
            act.wait_ge(q_stored[1], 32 * (NU // 2 - 1))
            last_high(0, ps_s[0], last_k_h, 1.0 / WS, last_k_ready, last_k_hi)
            last_high(1, ps_s[0], last_k_h, 1.0 / WS, last_k_ready, last_k_hi)
            last_high(0, ps_s[1], last_q_h, SC / WS, last_q_ready, last_q_hi)
            last_high(1, ps_s[1], last_q_h, SC / WS, last_q_ready, last_q_hi)
            copy_max(0, 0, None)
            for h in range(2):
                act.wait_ge(last_v_ready, 2 * h + 2)
                nc.scalar.activation(v_all[:, TILES - 4 + 2 * h:TILES - 2 + 2 * h, :].rearrange("p t n -> p (t n)"),
                                     ps_s[0][:, h].rearrange("p a b -> p (a b)"), ACT.Copy, scale=1.0 / WS).then_inc(last_v_copied, 1)
            walk_batches(act, 2, step)

            first_xt_whole()
            walk_units(act, unit_step)

        @block.tensor
        def _(pe):
            def score_for_max(b, r, turn, p, first, halves=(0, 1)):
                if p == 0 and 0 in halves:
                    pe.wait_ge(qk_loaded[r], 16 * QK_DMAS * (turn + 1))
                for h in halves:
                    if not (first and p == 0):
                        pe.wait_ge(half_reduced, H * b + 2 * p + h - 1)
                    nc.tensor.matmul(ps_m[h].rearrange("q e k -> q (e k)"), q_stack[r][0:ROW_MAX, p, P * h:P * (h + 1)],
                                     k_stack[r][0:ROW_MAX, p, :, :].rearrange("r e k -> r (e k)"),
                                     start=True, stop=True).then_inc(half_scored, 1)

            def score_pair(b, r, turn, p, first):
                if p == 0:
                    pe.wait_ge(max_loaded[r], 16 * (turn + 1))
                if not (first and p < 2):
                    pe.wait_ge(pair_exp, PAIRS * b + p - 1)
                for e in range(2):
                    for k in range(2):
                        last = nc.tensor.matmul(ps_s[p % 2][:, e, k, :], k_stack[r][:, p, e, P * k:P * (k + 1)],
                                                q_stack[r][:, p, :], start=True, stop=True)
                last.then_inc(pair_scored, 1)

            def weigh_values(b, r, g, first):
                if g == 0:
                    pe.wait_ge(v_padded, b + 1)
                pe.wait_ge(pair_exp, PAIRS * b + 2 * g + 2)
                if not (first and g == 0):
                    pe.wait_ge(pv_copied, GROUPS * b + g)
                for k in range(2):
                    for h in range(4):
                        last = nc.tensor.matmul(ps_o[32 * h:32 * h + 32, 0:N], v_pad[r][:, k, 4 * g + h, :],
                                                probs[g % 2][:, h // 2, h % 2, k, :], start=(k == 0), stop=(k == 1))
                last.then_inc(pv_ready, 1)

            def transpose_max(b, r):
                pe.wait_ge(half_reduced, H * b + H)
                if not (isinstance(b, int) and b == 0):
                    pe.wait_ge(max_copied, b)
                nc.tensor.transpose(ps_o[:, N:N + P], neg_max[r % 2][:], ident[:]).then_inc(max_transposed, 1)

            def back(b, h):
                if h == 0:
                    pe.wait_ge(pv_copied, GROUPS * b + GROUPS)
                else:
                    pe.wait_ge(normed, 2 * b + 1)
                for g in range(GROUPS):
                    last = nc.tensor.transpose(ps_c[:, P * g:P * (g + 1)], o_t[:, g, P * h:P * (h + 1)], ident[:])
                last.then_inc(back_ready, 1)

            def transpose_o(b):
                pe.wait_ge(normed, 2 * b + 2)
                for k in range(DK):
                    for h in range(2):
                        last = nc.tensor.transpose(ps_c[:, N * k + P * h:N * k + P * (h + 1)],
                                                   o_n[h][:, PAIRS * k:PAIRS * (k + 1), :].rearrange("p h d -> p (h d)"), ident[:])
                last.then_inc(ot_ready, 1)

            def project_o(b, halves=(0, 1)):
                if 0 in halves:
                    pe.wait_ge(ot_lo, b + 1)
                for h in halves:
                    for n, (o, w) in enumerate(((ot_h, wo_h), (ot_h, wo_l), (ot_l, wo_h))):
                        for k in range(DK):
                            last = nc.tensor.matmul(ps_c[:, D * h:D * (h + 1)], o[:, k, P * h:P * (h + 1)], w[:, k, :],
                                                    start=(n + k == 0), stop=(n == 2 and k == DK - 1))
                if 1 in halves:
                    last.then_inc(wo_ready, 1)

            def maxima(i, r, turn, has, p, h):
                if p < 4 and has(1):
                    score_for_max(i + 1, (r + 1) % RING, turn(1), p + 4, False, (h,))
                if p >= 4 and has(2):
                    score_for_max(i + 2, (r + 2) % RING, turn(2), p - 4, False, (h,))

            def step(i, r, turn, has):
                for p in range(PAIRS):
                    maxima(i, r, turn, has, p, 0)
                    score_pair(i, r % RING, turn(0), p, not has(-1))
                    maxima(i, r, turn, has, p, 1)
                    if p == 0 and has(-1):
                        weigh_values(i - 1, (r - 1) % RING, 3, False)
                    if p in (1, 2) and has(-1):
                        if p == 1:
                            pe.wait_ge(res_done, i - 1)
                        back(i - 1, p - 1)
                    if p == 3 and has(-1):
                        transpose_o(i - 1)
                    if p == 4 and has(1):
                        pe.wait_ge(pv_copied, GROUPS * i + 1)
                        transpose_max(i + 1, (r + 1) % RING)
                    if p in (5, 7) and has(-1):
                        project_o(i - 1, (p // 2 - 2,))
                    if p in (2, 4, 6) and has(0):
                        weigh_values(i, r % RING, p // 2 - 1, not has(-1))
                    if p == 4 and not has(1):
                        pe.wait_ge(half_reduced, H * B)
                        transpose_x(0, 0, True)

            def transpose_x(u, s, first):
                pe.wait_ge(xn_done, u + 1)
                if not first:
                    pe.wait_ge(xt_lo, u)
                    pe.wait_ge(xt_full, u)
                for k in range(DK):
                    for t in range(UT):
                        last = nc.tensor.transpose(ps_x[:, k, P * t:P * (t + 1)], xn[s][:, t, P * k:P * (k + 1)], ident[:])
                last.then_inc(xt_ready, 1)

            def gate_up(u, s, f, first, split):
                if f == 0:
                    pe.wait_ge(xt_lo, u + 1)
                    if not split:
                        pe.wait_ge(xt_full, u + 1)
                if first and f < 2:
                    pe.wait_ge(pair_exp, PAIRS * B - 1 + f)
                else:
                    pe.wait_ge(hid_done, FT * u + f - 1)
                for n, ps in ((0, ps_g), (1, ps_u)):
                    terms = [(w16[n], xt_h[s]), (w16[n], xt_l[s])] if split else [(w32[n], xt_f[s])]
                    for m, (w, v) in enumerate(terms):
                        for k in range(DK):
                            last = nc.tensor.matmul(ps[f % 2], w[:, k, P * f:P * (f + 1)], v[:, k, :],
                                                    start=(m + k == 0), stop=(m == len(terms) - 1 and k == DK - 1))
                last.then_inc(gu_ready, 1)

            def down(u, s, first, split):
                pe.wait_ge(hid_lo, FT * u + FT)
                if first:
                    pe.wait_ge(res_done, B)
                else:
                    pe.wait_ge(y_done, u)
                terms = [(hid_h[s], w16[2]), (hid_l[s], w16[2])] if split else [(hid_f[s], w32[2])]
                for t in range(UT):
                    for m, (v, w) in enumerate(terms):
                        for f in range(FT):
                            last = nc.tensor.matmul(ps_y[:, t, :], v[:, f, P * t:P * (t + 1)], w[:, f, :],
                                                    start=(m + f == 0), stop=(m == len(terms) - 1 and f == FT - 1))
                last.then_inc(y_ready, 1)

            def down_last(u, s, split):
                pe.wait_ge(y_done, u)
                terms = [(hid_h[s], w16[2]), (hid_l[s], w16[2])] if split else [(hid_f[s], w32[2])]

                def products(t, parts):
                    for f in parts:
                        for m, (v, w) in enumerate(terms):
                            last = nc.tensor.matmul(ps_y[:, t, :], v[:, f, P * t:P * (t + 1)], w[:, f, :],
                                                    start=(m + f == 0), stop=(m == len(terms) - 1 and f == FT - 1))
                    return last

                pe.wait_ge(hid_lo, FT * u + FT - 1)
                for t in (0, 2):
                    products(t, range(FT - 1))
                pe.wait_ge(hid_lo, FT * u + FT)
                products(0, (FT - 1,))
                products(1, range(FT)).then_inc(y_ready, 1)
                products(2, (FT - 1,))
                products(3, range(FT)).then_inc(y_ready, 1)

            def whole(split):
                def unit_step(u, s, has):
                    for f in range(FT):
                        gate_up(u, s, f, not has(-1), split)
                        if f == 2 and has(1):
                            transpose_x(u + 1, 1 - s, False)
                        if f == 3 and has(-1):
                            down(u - 1, 1 - s, not has(-2), split)
                        if not has(-1):
                            if f == 0:
                                weigh_values(B - 1, (B - 1) % RING, GROUPS - 1, False)
                            if f == 1:
                                pe.wait_ge(res_done, B - 1)
                                back(B - 1, 0)
                            if f == 2:
                                back(B - 1, 1)
                            if f == 3:
                                transpose_o(B - 1)
                            if f == 5:
                                project_o(B - 1)

                walk_units(pe, unit_step)
                down_last(NU - 1, 1, split)

            def last_v(t):
                for n, (w, v, k, rows) in enumerate(ctx_terms(wv_h, wv_l, last_ctx_h, last_ctx_l)):
                    last = nc.tensor.matmul(ps_s[0][:, t // 2, t % 2, :],
                                            v[0:rows, k, P * t:P * (t + 1)], w[0:rows, k, :],
                                            start=(n == 0), stop=(n == CTX_TERMS - 1))
                last.then_inc(last_v_ready, 1)

            def last_k(part):
                e, second = part // 2, part % 2
                for n in range(3 * second, 3 + 2 * second):
                    w, v, k, rows = ctx_terms(wk_h, wk_l, last_ctx_h, last_ctx_l)[n]
                    last = nc.tensor.matmul(ps_s[0][:, e].rearrange("p b t -> p (b t)"),
                                            w[0:rows, k, P * e:P * (e + 1)], v[0:rows, k, :],
                                            start=(n == 0), stop=(n == CTX_TERMS - 1))
                if second:
                    last.then_inc(last_k_ready, 1)

            def last_q(part):
                e, second = part // 2, part % 2
                products = [(w, v, k) for w, v in ((wq_h, last_xt_h), (wq_l, last_xt_h), (wq_h, last_xt_l))
                            for k in range(DK)]
                for n in range(3 * second, 3 * second + 3):
                    w, v, k = products[n]
                    last = nc.tensor.matmul(ps_s[1][:, e].rearrange("p b t -> p (b t)"),
                                            w[:, k, P * e:P * (e + 1)], v[:, k, :], start=(n == 0), stop=(n == 5))
                if second:
                    last.then_inc(last_q_ready, 1)

            for n in range(PAIRS + 4):
                if n == PAIRS:
                    pe.wait_ge(last_k_lo, 2)
                (last_k, last_q, last_v)[n // 4](n % 4)
                if n == PAIRS + 1:
                    transpose_max(0, 0)
                score_for_max(n // PAIRS, n // PAIRS, 0, n % PAIRS, n < PAIRS)
            pe.wait_ge(last_q_lo, 2)
            pe.wait_ge(last_v_copied, 2)
            pe.wait_ge(ones_loaded, 16 * RING)
            walk_batches(pe, 2, step)

            large = pe.value_load(w_large[0:1, 0:1], min_val=0, max_val=1)
            with pe.If(large == 0):
                whole(True)
            with pe.Else():
                pe.wait_ge(w32_made, 3)
                whole(False)


def kernel(**inputs):
    import numpy as _np
    import concourse.bacc as _bacc
    from concourse import mybir as _mybir
    from concourse.bass_utils import run_bass_kernel_spmd as _run

    def by_row(w):
        return _np.asarray(w).reshape(-1, PAIRS, 2, HD).transpose(0, 2, 3, 1).reshape(-1, H * HD)

    arrays = {
        "x": _np.asarray(inputs["x"]).reshape(B * N, D),
        "ctx_t": _np.asarray(inputs["ctx_768"]).transpose(2, 0, 1).reshape(C, B * N),
        "wq": by_row(inputs["L0_xattn_Wq"]),
        "wk": by_row(inputs["L0_xattn_Wk"]),
        "wv": inputs["L0_xattn_Wv"],
        "wo": inputs["L0_xattn_Wo"],
        "bo": inputs["L0_xattn_bo"],
        "wg": _np.asarray(inputs["L0_ffn_w_gate"]).T,
        "wu": _np.asarray(inputs["L0_ffn_w_up"]).T,
        "wd": _np.asarray(inputs["L0_ffn_w_down"]).T,
    }
    arrays = {f"in_{k}": _np.ascontiguousarray(v) for k, v in arrays.items()}
    nc = _bacc.Bacc("TRN2", target_bir_lowering=False, num_devices=1)
    args = [nc.dram_tensor(k, a.shape, _mybir.dt.from_np(a.dtype), kind="ExternalInput").ap()
            for k, a in arrays.items()]
    out = nc.dram_tensor("out_0_dram", (B * N, D), _mybir.dt.float32, kind="ExternalOutput").ap()
    block_program(nc, *args, out)
    r = _run(nc, [arrays], core_ids=[0])
    return r.results[0]["out_0_dram"].reshape(B, N, D)
```
